# Optimizing a Trainium2 kernel written in Bass

```python
import numpy as np
import jax
import jax.numpy as jnp

def _softmax(x, axis=-1):
    return jax.nn.softmax(x, axis=axis)

def _gelu(x):
    return jax.nn.gelu(x, approximate=True)

def _silu(x):
    return jax.nn.silu(x)

def _sigmoid(x):
    return jax.nn.sigmoid(x)

def _layernorm(x, axis=-1, eps=1e-05):
    m = jnp.mean(x, axis=axis, keepdims=True)
    v = jnp.var(x, axis=axis, keepdims=True)
    return (x - m) / jnp.sqrt(v + eps)

def _scatter_add(tgt, idx, src, axis=0):
    return tgt.at[idx].add(src)

def _segment_sum(src, seg, n):
    return jax.ops.segment_sum(src, seg, n)
kernel_name = 'mk_adaln_d1_jaxref_r8_8fe42e'

def setup_inputs(seed: int=0):
    np.random.seed(seed)
    _w = jnp.asarray

    def _L0_attn_setup():
        import jax, jax.numpy as jnp
        import numpy as np
        B, S, D = (2, 256, 256)
        H, HD = (32, 128)
        P = H * HD
        K = 4
        F_ = 1024
        EPS = 1e-06

        def _rmsnorm(x, w, eps=EPS):
            xf = x.astype(jnp.float32)
            y = xf * jax.lax.rsqrt(jnp.mean(xf * xf, axis=-1, keepdims=True) + eps)
            return (y * w).astype(x.dtype)

        def _short_conv(x, w):
            k = w.shape[1]
            xp = jnp.pad(x, ((0, 0), (k - 1, 0), (0, 0)))
            y = sum((xp[:, j:j + x.shape[1], :] * w[:, j] for j in range(k)))
            return jax.nn.silu(y)

        def _l2norm(x, eps=1e-06):
            return x * jax.lax.rsqrt(jnp.sum(x * x, axis=-1, keepdims=True) + eps)

        def _kda(q, k, v, g, beta):
            scale = q.shape[-1] ** (-0.5)
            q = _l2norm(q) * scale
            k = _l2norm(k)
            tm = lambda a: jnp.swapaxes(a, 0, 1)
            qs, ks_, vs, gs, bs = (tm(q), tm(k), tm(v), tm(g), tm(beta))
            bsz, h, hd = (q.shape[0], q.shape[2], q.shape[3])
            S0 = jnp.zeros((bsz, h, hd, hd), jnp.float32)

            def step(St, inp):
                qt, kt, vt, gt, bt = inp
                St = St * jnp.exp(gt)[..., None]
                err = jnp.einsum('bhk,bhkv->bhv', kt, St)
                St = St + bt[..., None, None] * kt[..., None] * (vt - err)[..., None, :]
                ot = jnp.einsum('bhk,bhkv->bhv', qt, St)
                return (St, ot)
            _, o = jax.lax.scan(step, S0, (qs, ks_, vs, gs, bs))
            return jnp.swapaxes(o, 0, 1)
        key = jax.random.key(seed)
        ks = jax.random.split(key, 20)
        std = 0.02
        inp = {'x': jax.random.normal(ks[0], (B, S, D), jnp.float32), 'norm1_w': jnp.ones((D,), jnp.float32), 'wq': jax.random.normal(ks[1], (D, P), jnp.float32) * std, 'wk': jax.random.normal(ks[2], (D, P), jnp.float32) * std, 'wv': jax.random.normal(ks[3], (D, P), jnp.float32) * std, 'conv_q': jax.random.normal(ks[4], (P, K), jnp.float32) * 0.5, 'conv_k': jax.random.normal(ks[5], (P, K), jnp.float32) * 0.5, 'conv_v': jax.random.normal(ks[6], (P, K), jnp.float32) * 0.5, 'f_a': jax.random.normal(ks[7], (D, HD), jnp.float32) * std, 'f_b': jax.random.normal(ks[8], (HD, P), jnp.float32) * std, 'A_log': jnp.log(jax.random.uniform(ks[9], (H,), jnp.float32, 1.0, 16.0)), 'dt_bias': jnp.zeros((P,), jnp.float32), 'b_w': jax.random.normal(ks[10], (D, H), jnp.float32) * std, 'g_a': jax.random.normal(ks[11], (D, HD), jnp.float32) * std, 'g_b': jax.random.normal(ks[12], (HD, P), jnp.float32) * std, 'onorm_w': jnp.ones((HD,), jnp.float32), 'wo': jax.random.normal(ks[13], (P, D), jnp.float32) * std, 'norm2_w': jnp.ones((D,), jnp.float32), 'w1': jax.random.normal(ks[14], (D, F_), jnp.float32) * std, 'w2': jax.random.normal(ks[15], (F_, D), jnp.float32) * std, 'w3': jax.random.normal(ks[16], (D, F_), jnp.float32) * std}
        return inp
    _L0_attn_in = _L0_attn_setup()

    def _L0_ffn_setup():
        import jax, jax.numpy as jnp
        import numpy as np
        B, S, D, H = (4, 256, 256, 1024)

        def fwht(x):
            orig_shape = x.shape
            n = orig_shape[-1]
            x = x.reshape(-1, n)
            h = 1
            while h < n:
                xb = x.reshape(-1, n // (2 * h), 2, h)
                a = xb[:, :, 0, :]
                b = xb[:, :, 1, :]
                x = jnp.stack([a + b, a - b], axis=2).reshape(-1, n)
                h *= 2
            scale = jnp.asarray(1.0 / np.sqrt(n), dtype=x.dtype)
            return (x * scale).reshape(orig_shape)
        key = jax.random.key(seed)
        kx, k1, k2, k3 = jax.random.split(key, 4)
        x = jax.random.normal(kx, (B, S, D), dtype=jnp.float32)
        W1 = jax.random.normal(k1, (H, D), dtype=jnp.float32) * (1.0 / np.sqrt(D))
        W2 = jax.random.normal(k2, (D, H), dtype=jnp.float32) * (1.0 / np.sqrt(H))
        W3 = jax.random.normal(k3, (H, D), dtype=jnp.float32) * (1.0 / np.sqrt(D))
        return {'x': x, 'W1': W1, 'W2': W2, 'W3': W3}
    _L0_ffn_in = _L0_ffn_setup()
    _L0_c = _w((lambda *s: np.random.randn(*s).astype(np.float32) * 0.05)(2, 256))
    _L0_wmod = _w((lambda *s: np.random.randn(*s).astype(np.float32) * 0.05)(256, 6 * 256) * 256 ** (-0.5))
    _d = {'L0_attn_x': _L0_attn_in['x'], 'L0_attn_norm1_w': _L0_attn_in['norm1_w'], 'L0_attn_wq': _L0_attn_in['wq'], 'L0_attn_wk': _L0_attn_in['wk'], 'L0_attn_wv': _L0_attn_in['wv'], 'L0_attn_conv_q': _L0_attn_in['conv_q'], 'L0_attn_conv_k': _L0_attn_in['conv_k'], 'L0_attn_conv_v': _L0_attn_in['conv_v'], 'L0_attn_f_a': _L0_attn_in['f_a'], 'L0_attn_f_b': _L0_attn_in['f_b'], 'L0_attn_A_log': _L0_attn_in['A_log'], 'L0_attn_dt_bias': _L0_attn_in['dt_bias'], 'L0_attn_b_w': _L0_attn_in['b_w'], 'L0_attn_g_a': _L0_attn_in['g_a'], 'L0_attn_g_b': _L0_attn_in['g_b'], 'L0_attn_onorm_w': _L0_attn_in['onorm_w'], 'L0_attn_wo': _L0_attn_in['wo'], 'L0_attn_norm2_w': _L0_attn_in['norm2_w'], 'L0_attn_w1': _L0_attn_in['w1'], 'L0_attn_w2': _L0_attn_in['w2'], 'L0_attn_w3': _L0_attn_in['w3'], 'L0_ffn_W1': _L0_ffn_in['W1'], 'L0_ffn_W2': _L0_ffn_in['W2'], 'L0_ffn_W3': _L0_ffn_in['W3'], 'L0_c': _L0_c, 'L0_wmod': _L0_wmod}
    _x0 = _d['L0_attn_x']
    _d['L0_attn_x'] = jax.random.normal(jax.random.fold_in(jax.random.key(seed), 1), (2, 2048, 256), dtype=_x0.dtype)
    del _x0
    return _d

def reference(L0_attn_x, L0_attn_norm1_w, L0_attn_wq, L0_attn_wk, L0_attn_wv, L0_attn_conv_q, L0_attn_conv_k, L0_attn_conv_v, L0_attn_f_a, L0_attn_f_b, L0_attn_A_log, L0_attn_dt_bias, L0_attn_b_w, L0_attn_g_a, L0_attn_g_b, L0_attn_onorm_w, L0_attn_wo, L0_attn_norm2_w, L0_attn_w1, L0_attn_w2, L0_attn_w3, L0_ffn_W1, L0_ffn_W2, L0_ffn_W3, L0_c, L0_wmod):

    def _L0_attn_ref(x, norm1_w, wq, wk, wv, conv_q, conv_k, conv_v, f_a, f_b, A_log, dt_bias, b_w, g_a, g_b, onorm_w, wo, norm2_w, w1, w2, w3):
        import jax, jax.numpy as jnp
        import numpy as np
        B, S, D = (2, 256, 256)
        H, HD = (32, 128)
        P = H * HD
        K = 4
        F_ = 1024
        EPS = 1e-06

        def _rmsnorm(x, w, eps=EPS):
            xf = x.astype(jnp.float32)
            y = xf * jax.lax.rsqrt(jnp.mean(xf * xf, axis=-1, keepdims=True) + eps)
            return (y * w).astype(x.dtype)

        def _short_conv(x, w):
            k = w.shape[1]
            xp = jnp.pad(x, ((0, 0), (k - 1, 0), (0, 0)))
            y = sum((xp[:, j:j + x.shape[1], :] * w[:, j] for j in range(k)))
            return jax.nn.silu(y)

        def _l2norm(x, eps=1e-06):
            return x * jax.lax.rsqrt(jnp.sum(x * x, axis=-1, keepdims=True) + eps)

        def _kda(q, k, v, g, beta):
            scale = q.shape[-1] ** (-0.5)
            q = _l2norm(q) * scale
            k = _l2norm(k)
            tm = lambda a: jnp.swapaxes(a, 0, 1)
            qs, ks_, vs, gs, bs = (tm(q), tm(k), tm(v), tm(g), tm(beta))
            bsz, h, hd = (q.shape[0], q.shape[2], q.shape[3])
            S0 = jnp.zeros((bsz, h, hd, hd), jnp.float32)

            def step(St, inp):
                qt, kt, vt, gt, bt = inp
                St = St * jnp.exp(gt)[..., None]
                err = jnp.einsum('bhk,bhkv->bhv', kt, St)
                St = St + bt[..., None, None] * kt[..., None] * (vt - err)[..., None, :]
                ot = jnp.einsum('bhk,bhkv->bhv', qt, St)
                return (St, ot)
            _, o = jax.lax.scan(step, S0, (qs, ks_, vs, gs, bs))
            return jnp.swapaxes(o, 0, 1)
        bsz, seq, _ = x.shape
        h = _rmsnorm(x, norm1_w)
        q = _short_conv(h @ wq, conv_q).reshape(bsz, seq, H, HD)
        k = _short_conv(h @ wk, conv_k).reshape(bsz, seq, H, HD)
        v = _short_conv(h @ wv, conv_v).reshape(bsz, seq, H, HD)
        g = (h @ f_a @ f_b).reshape(bsz, seq, H, HD).astype(jnp.float32)
        g = g + dt_bias.reshape(H, HD)
        g = -jnp.exp(A_log)[:, None] * jax.nn.softplus(g)
        beta = jax.nn.sigmoid((h @ b_w).astype(jnp.float32))
        o = _kda(q.astype(jnp.float32), k.astype(jnp.float32), v.astype(jnp.float32), g, beta)
        gate = (h @ g_a @ g_b).reshape(bsz, seq, H, HD)
        og = o * jax.nn.sigmoid(gate.astype(jnp.float32))
        og = og * jax.lax.rsqrt(jnp.mean(og * og, axis=-1, keepdims=True) + EPS)
        o = (og * onorm_w).astype(x.dtype).reshape(bsz, seq, P)
        x = x + o @ wo
        h2 = _rmsnorm(x, norm2_w)
        ffn = jax.nn.silu(h2 @ w1) * (h2 @ w3) @ w2
        return x + ffn

    def _L0_ffn_ref(x, W1, W2, W3):
        import jax, jax.numpy as jnp
        import numpy as np
        B, S, D, H = (4, 256, 256, 1024)

        def fwht(x):
            orig_shape = x.shape
            n = orig_shape[-1]
            x = x.reshape(-1, n)
            h = 1
            while h < n:
                xb = x.reshape(-1, n // (2 * h), 2, h)
                a = xb[:, :, 0, :]
                b = xb[:, :, 1, :]
                x = jnp.stack([a + b, a - b], axis=2).reshape(-1, n)
                h *= 2
            scale = jnp.asarray(1.0 / np.sqrt(n), dtype=x.dtype)
            return (x * scale).reshape(orig_shape)
        up_gate = jnp.einsum('bsd,hd->bsh', x, W1)
        up_lin = jnp.einsum('bsd,hd->bsh', x, W3)
        hidden = jax.nn.silu(up_gate) * up_lin
        hidden = fwht(hidden)
        out = jnp.einsum('bsh,dh->bsd', hidden, W2)
        return out
    x = L0_attn_x
    mod = (_silu(L0_c) @ L0_wmod).reshape(L0_c.shape[0], 6, 1, -1)
    sa, ca, ga, sb, cb, gb = (mod[:, 0], mod[:, 1], mod[:, 2], mod[:, 3], mod[:, 4], mod[:, 5])
    ga = (2 * (ga >= 0) - 1) * jnp.maximum(jnp.abs(ga), 0.25)
    gb = (2 * (gb >= 0) - 1) * jnp.maximum(jnp.abs(gb), 0.25)
    h = _layernorm(x, axis=-1) * (1 + ca) + sa
    x = x + ga * _L0_attn_ref(h, L0_attn_norm1_w, L0_attn_wq, L0_attn_wk, L0_attn_wv, L0_attn_conv_q, L0_attn_conv_k, L0_attn_conv_v, L0_attn_f_a, L0_attn_f_b, L0_attn_A_log, L0_attn_dt_bias, L0_attn_b_w, L0_attn_g_a, L0_attn_g_b, L0_attn_onorm_w, L0_attn_wo, L0_attn_norm2_w, L0_attn_w1, L0_attn_w2, L0_attn_w3)
    h = _layernorm(x, axis=-1) * (1 + cb) + sb
    x = x + gb * _L0_ffn_ref(h, L0_ffn_W1, L0_ffn_W2, L0_ffn_W3)
    return x

_drawn_inputs = setup_inputs


def setup_inputs(seed=0):
    import zlib

    import numpy as np

    out = dict(_drawn_inputs(seed))
    spreads = {'L0_attn_norm1_w': (1.0, 0.2),
     'L0_attn_dt_bias': (0.0, 0.8),
     'L0_attn_onorm_w': (1.0, 0.6),
     'L0_attn_norm2_w': (1.0, 0.6)}
    factors = {'L0_attn_f_a': 8.0,
     'L0_attn_f_b': 8.0,
     'L0_attn_A_log': 3.823,
     'L0_attn_b_w': 4.265,
     'L0_attn_g_a': 8.0,
     'L0_attn_g_b': 8.0,
     'L0_attn_w1': 6.049,
     'L0_attn_w2': 5.971,
     'L0_attn_w3': 5.98}
    for name, (base, spread) in spreads.items():
        noise = np.random.default_rng([zlib.crc32(name.encode()), seed]).standard_normal(out[name].shape)
        drawn = base * np.exp(spread * noise) if base else spread * noise
        out[name] = jnp.asarray(drawn.astype(out[name].dtype))
    for name, factor in factors.items():
        out[name] = (out[name] * factor).astype(out[name].dtype)
    return out
```

```python
from contextlib import ExitStack

import concourse.bass as bass
from concourse import mybir

F32 = mybir.dt.float32
I32 = mybir.dt.int32
ALU = mybir.AluOpType
ACT = mybir.ActivationFunctionType

P = 128
PAIR = 2
LEVELS = 7
KS = 4
GROUP = 512
LN_EXP = "natural_log_exp_and_others"
QK_SCALE = 2.0 ** 32
ROUND = 2.0 ** -40
SOFTPLUS_MAX = 40.0


def adaln_kernel(nc, x, norm1_w, wq, wk, wv, conv_q, conv_k, conv_v, f_a, f_b, A_log, dt_bias,
                 b_w, g_a, g_b, onorm_w, wo, norm2_w, w1, w2, w3, W1, W2, W3, c, wmod, masks_in,
                 out):
    B, S, D = x.shape
    HTOT = A_log.shape[0]
    FF = w1.shape[1]
    KD = D // P
    NT = S // P
    NP = HTOT // PAIR
    C = B * PAIR
    NG = B * S // GROUP
    GB = S // GROUP
    SUB = GROUP // P
    FT = FF // P
    HALF = P // 2
    N_STEPS = NP * NT
    assert (B, D, f_a.shape[1]) == (2, 256, P) and C * P == 512 and S % GROUP == 0

    ctx = ExitStack()
    with ctx:
        def sb(where, name, shape):
            return where.enter_context(nc.sbuf_tensor(name, shape, F32))

        in_use = []

        def sem(name):
            in_use.append(nc.alloc_semaphore(name=name))
            return in_use[-1]

        def end_phase():
            nc.all_engine_barrier()
            nc.clear_and_free_semaphores(list(in_use))
            nc.all_engine_barrier()
            in_use.clear()

        bank = [ctx.enter_context(nc.psum_tensor(f"bank{i}", [P, 512], F32)) for i in range(8)]

        ident = sb(ctx, "ident", [P, P])
        ones = sb(ctx, "ones", [P, P])
        eps6 = sb(ctx, "eps6", [P, 1])
        eps5 = sb(ctx, "eps5", [P, 1])
        qscale = sb(ctx, "qscale", [P, 1])
        mod = sb(ctx, "mod", [P, 6 * KD, B])
        Y = sb(ctx, "Y", [P, KD, B * S])
        modv = mod[:, :, :].rearrange("p (v k) b -> p v k b", v=6)
        SA, CA, GA, SB_, CB, GBv = range(6)

        mid = ExitStack()
        hn = sb(mid, "hn", [P, KD, B * S])
        hfa = sb(mid, "hfa", [P, B * S])
        hga = sb(mid, "hga", [P, B * S])
        beta = sb(mid, "beta", [P, B * NT, HTOT])
        negA = sb(mid, "negA", [P, HTOT])
        masks = sb(mid, "masks", [P, LEVELS, HALF])
        keep = sb(mid, "keep", [P, NT])
        onw = sb(mid, "onw", [P, 1])

        with ExitStack() as ph:
            xs = sb(ph, "xs", [P, B * S // P, D])
            wm = sb(ph, "wm", [P, KD, 6 * D])
            fa_s = sb(ph, "fa_s", [P, KD, P])
            ga_s = sb(ph, "ga_s", [P, KD, P])
            bw_s = sb(ph, "bw_s", [P, KD, HTOT])
            n1 = sb(ph, "n1", [P, KD])
            cT = sb(ph, "cT", [P, KD, B])
            sgn = sb(ph, "sgn", [P, KD, B])
            mag = sb(ph, "mag", [P, KD, B])
            stats = sb(ph, "stats", [P, SUB, 6])
            mv = sb(ph, "mv", [P, SUB, 2])
            rs = sb(ph, "rs", [P, SUB])
            xh = sb(ph, "xh", [P, SUB, D])
            sq = sb(ph, "sq", [P, KD, GROUP])
            rr = sb(ph, "rr", [P, GROUP])
            bT = sb(ph, "bT", [HTOT, GROUP])
            b1 = sb(ph, "b1", [P, SUB, HTOT])

            load_c = sem("load_c")
            load_x = sem("load_x")
            load_w = sem("load_w")
            consts = sem("consts")
            silu_c = sem("silu_c")
            mod_mm = sem("mod_mm")
            mod_cp = sem("mod_cp")
            mod_steps = sem("mod_steps")
            negA_e = sem("negA_e")
            st_bn = sem("st_bn")
            st_mv = sem("st_mv")
            st_ln = sem("st_ln")
            st_rs = sem("st_rs")
            x_hat = sem("x_hat")
            x_tr = sem("x_tr")
            h_done = sem("h_done")
            h_sq = sem("h_sq")
            ss_mm = sem("ss_mm")
            ss_ln = sem("ss_ln")
            ss_rs = sem("ss_rs")
            hn_done = sem("hn_done")
            low_mm = sem("low_mm")
            b_mm = sem("b_mm")
            fa_cp = sem("fa_cp")
            ga_cp = sem("ga_cp")
            b_exp = sem("b_exp")
            b_tr = sem("b_tr")
            b_add = sem("b_add")
            b_done = sem("b_done")

            waited = sem("waited")
            N_C = 16 * 3
            N_W = 16 * 8

            with nc.Block() as block:
                @block.sync
                def _(eng):
                    with nc.allow_non_contiguous_dma("a few vectors, once"):
                        for b in range(B):
                            eng.dma_start(cT[:, :, b], c[b, :].rearrange("(k p) -> p k", p=P)).then_inc(load_c, 16)
                        eng.dma_start(wm[:, :, :], wmod.rearrange("(k p) n -> p k n", p=P)).then_inc(load_c, 16)
                        eng.dma_start(n1[:, :], norm1_w.rearrange("(k p) -> p k", p=P)).then_inc(load_w, 16)
                        eng.dma_start(onw[:, :], onorm_w.rearrange("(p a) -> p a", a=1)).then_inc(load_w, 16)
                        eng.dma_start(negA[:, :], A_log.rearrange("(a h) -> a h", a=1).broadcast_to([P, HTOT])).then_inc(load_w, 16)
                        for s_, d_ in ((fa_s, f_a), (ga_s, g_a), (bw_s, b_w)):
                            eng.dma_start(s_[:, :, :], d_.rearrange("(k p) n -> p k n", p=P)).then_inc(load_w, 16)
                        eng.dma_start(keep[:, :], masks_in[:, P + LEVELS * HALF:]).then_inc(load_w, 16)
                        eng.dma_start(masks[:, :, :], masks_in[:, P:P + LEVELS * HALF].rearrange("p (l n) -> p l n", l=LEVELS)).then_inc(load_w, 16)

                @block.gpsimd
                def _(eng):
                    eng.dma_start(ident[:, :], masks_in[:, 0:P]).then_inc(load_x, 16)
                    for b in range(B):
                        eng.dma_start(xs[:, b * NT:(b + 1) * NT, :],
                                      x[b, :, :].rearrange("(t p) d -> p t d", p=P)).then_inc(load_x, 16)
                    eng.memset(ones[:, :], 1.0).then_inc(consts, 1)
                    eng.memset(eps6[:, :], 1e-6).then_inc(consts, 1)
                    eng.memset(eps5[:, :], 1e-5).then_inc(consts, 1)
                    eng.memset(qscale[:, :], float(-0.5 * 4.852030263919617 - 0.6931471805599453)).then_inc(consts, 1)

                @block.tensor
                def _(eng):
                    eng.wait_ge(load_c, N_C)
                    eng.wait_ge(silu_c, 1)
                    for j in range(6 * KD):
                        for k in range(KD):
                            mm = eng.matmul(bank[7][:, j * B:(j + 1) * B], wm[:, k, j * P:(j + 1) * P],
                                            cT[:, k, :], start=(k == 0), stop=(k == KD - 1))
                    mm.then_inc(mod_mm, 1)
                    eng.wait_ge(load_w, N_W)
                    eng.wait_ge(load_x, 48)
                    eng.wait_ge(consts, 4)
                    with eng.Fori(0, NG) as g:
                        tok = bass.ds(g * GROUP, GROUP)
                        eng.wait_ge(x_hat, g + 1)
                        for k in range(KD):
                            for s in range(SUB):
                                mm = eng.transpose(bank[k][:, s * P:(s + 1) * P], xh[:, s, k * P:(k + 1) * P], ident[:, :])
                        mm.then_inc(x_tr, 1)
                        eng.wait_ge(h_sq, g + 1)
                        for k in range(KD):
                            mm = eng.matmul(bank[2][:, :], ones[:, :], sq[:, k, :], start=(k == 0), stop=(k == KD - 1))
                        mm.then_inc(ss_mm, 1)
                        eng.wait_ge(hn_done, g + 1)
                        for k in range(KD):
                            eng.matmul(bank[3][:, :], fa_s[:, k, :], hn[:, k, tok], start=(k == 0), stop=(k == KD - 1))
                        for k in range(KD):
                            mm = eng.matmul(bank[4][:, :], ga_s[:, k, :], hn[:, k, tok], start=(k == 0), stop=(k == KD - 1))
                        mm.then_inc(low_mm, 1)
                        for k in range(KD):
                            mm = eng.matmul(bank[5][0:HTOT, :], bw_s[:, k, :], hn[:, k, tok], start=(k == 0), stop=(k == KD - 1))
                        mm.then_inc(b_mm, 1)
                        eng.wait_ge(b_exp, g + 1)
                        eng.sem_inc(waited, 1)
                        for s in range(SUB):
                            mm = eng.transpose(bank[6][:, s * HTOT:(s + 1) * HTOT], bT[:, s * P:(s + 1) * P],
                                               ident[0:HTOT, 0:HTOT])
                        mm.then_inc(b_tr, 1)

                @block.scalar
                def _(eng):
                    eng.wait_ge(load_c, N_C)
                    eng.activation(cT[:, :, :], cT[:, :, :], ACT.Silu).then_inc(silu_c, 1)
                    eng.wait_ge(load_w, N_W)
                    eng.preload_act_table_set(LN_EXP)
                    eng.activation(negA[:, :], negA[:, :], ACT.Exp).then_inc(negA_e, 1)
                    eng.wait_ge(consts, 4)
                    eng.wait_ge(mod_steps, 5)
                    with eng.Fori(0, NG) as g:
                        tok = bass.ds(g * GROUP, GROUP)
                        half = bass.ds(g // GB, 1)
                        eng.wait_ge(st_mv, g + 1)
                        eng.activation(rs[:, :], mv[:, :, 1], ACT.Ln, bias=eps5[:, :]).then_inc(st_ln, 1)
                        eng.wait_ge(st_ln, g + 1)
                        eng.activation(rs[:, :], rs[:, :], ACT.Exp, scale=-0.5).then_inc(st_rs, 1)
                        eng.wait_ge(x_tr, g + 1)
                        for k in range(KD):
                            a = eng.activation(Y[:, k, tok], bank[k][:, :], ACT.Identity,
                                               bias=modv[:, SA, k, half], scale=modv[:, CA, k, half])
                        a.then_inc(h_done, 1)
                        eng.wait_ge(h_done, g + 1)
                        eng.sem_inc(waited, 1)
                        eng.activation(sq[:, :, :], Y[:, :, tok], ACT.Square).then_inc(h_sq, 1)
                        eng.wait_ge(ss_mm, g + 1)
                        eng.activation(rr[:, :], bank[2][:, :], ACT.Ln, bias=eps6[:, :], scale=1.0 / D).then_inc(ss_ln, 1)
                        eng.wait_ge(ss_ln, g + 1)
                        eng.activation(rr[:, :], rr[:, :], ACT.Exp, scale=-0.5).then_inc(ss_rs, 1)
                        eng.wait_ge(b_mm, g + 1)
                        eng.activation(bT[:, :], bank[5][0:HTOT, :], ACT.Exp, scale=-1.0).then_inc(b_exp, 1)
                        eng.activation(hfa[:, tok], bank[3][:, :], ACT.Copy).then_inc(fa_cp, 1)

                @block.vector
                def _(eng):
                    eng.wait_ge(mod_mm, 1)
                    eng.tensor_copy(mod[:, :, :], bank[7][:, 0:6 * KD * B].rearrange("p (j b) -> p j b", b=B)).then_inc(mod_cp, 1)
                    eng.wait_ge(mod_cp, 1)
                    n = 0
                    for v in (CA, CB):
                        eng.tensor_scalar(modv[:, v, :, :], modv[:, v, :, :], 1.0, None, ALU.add).then_inc(mod_steps, 1)
                        n += 1
                    for v in (GA, GBv):
                        gv = modv[:, v, :, :]
                        eng.tensor_scalar(sgn[:, :, :], gv, 0.0, 2.0, ALU.is_ge, ALU.mult).then_inc(mod_cp, 1)
                        eng.scalar_tensor_tensor(mag[:, :, :], gv, -1.0, gv, ALU.mult, ALU.max).then_inc(mod_cp, 1)
                        eng.wait_ge(mod_cp, 3 * (n - 2) + 3)
                        eng.tensor_scalar(mag[:, :, :], mag[:, :, :], 0.25, None, ALU.max).then_inc(mod_cp, 1)
                        eng.wait_ge(mod_cp, 3 * (n - 2) + 4)
                        eng.scalar_tensor_tensor(gv, sgn[:, :, :], -1.0, mag[:, :, :], ALU.add, ALU.mult).then_inc(mod_steps, 1)
                        n += 1
                        eng.wait_ge(mod_steps, n)
                    eng.wait_ge(negA_e, 1)
                    eng.tensor_scalar(negA[:, :], negA[:, :], -1.0, None, ALU.mult).then_inc(mod_steps, 1)
                    eng.wait_ge(load_x, 48)
                    with eng.Fori(0, NG) as g:
                        tok = bass.ds(g * GROUP, GROUP)
                        for s in range(SUB):
                            eng.bn_stats(stats[:, s, :], xs[:, bass.ds(g * SUB + s, 1), :]).then_inc(st_bn, 1)
                        eng.wait_ge(st_bn, (g + 1) * SUB)
                        eng.sem_inc(waited, 1)
                        for s in range(SUB):
                            a = eng.bn_aggr(mv[:, s, :], stats[:, s, :])
                        a.then_inc(st_mv, 1)
                        eng.wait_ge(st_mv, g + 1)
                        eng.wait_ge(st_rs, g + 1)
                        for s in range(SUB):
                            a = eng.tensor_scalar(xh[:, s, :], xs[:, bass.ds(g * SUB + s, 1), :],
                                                  mv[:, s, 0:1], rs[:, s:s + 1], ALU.subtract, ALU.mult)
                        a.then_inc(x_hat, 1)
                        eng.wait_ge(ss_rs, g + 1)
                        for k in range(KD):
                            a = eng.scalar_tensor_tensor(hn[:, k, tok], Y[:, k, tok], n1[:, k:k + 1], rr[:, :],
                                                         ALU.mult, ALU.mult)
                        a.then_inc(hn_done, 1)
                        eng.wait_ge(low_mm, g + 1)
                        eng.tensor_copy(hga[:, tok], bank[4][:, :]).then_inc(ga_cp, 1)
                        eng.wait_ge(b_tr, g + 1)
                        eng.tensor_scalar(b1[:, :, :], bank[6][:, 0:SUB * HTOT].rearrange("p (s h) -> p s h", h=HTOT),
                                          1.0, None, ALU.add).then_inc(b_add, 1)
                        eng.wait_ge(b_add, g + 1)
                        eng.reciprocal(beta[:, bass.ds(g * SUB, SUB), :], b1[:, :, :]).then_inc(b_done, 1)

        end_phase()

        with mid:
            w_qkv = sb(mid, "w_qkv", [P, 3, KD, PAIR * P])
            w_fb = sb(mid, "w_fb", [P, PAIR * P])
            w_gb = sb(mid, "w_gb", [P, PAIR * P])
            w_o = sb(mid, "w_o", [P, PAIR, D])
            cw = sb(mid, "cw", [P, 3, PAIR, KS])
            dtp = sb(mid, "dtp", [P, PAIR])

            def tile4(name):
                return sb(mid, name, [P, C, P])

            raw = sb(mid, "raw", [P, 3, C, P + KS - 1])
            acc = sb(mid, "acc", [P, 3, C, P])
            qk = sb(mid, "qk", [P, 2, C, P])
            qs, ks, vs = qk[:, 0, :, :], qk[:, 1, :, :], tile4("vs")
            zp, zc, u, r = tile4("zp"), tile4("zc"), tile4("u"), tile4("r")
            lnw = zc
            a = tile4("a")
            k2 = tile4("k2")
            lns = sb(mid, "lns", [P, 2 * C])
            cq_new = sb(mid, "cq_new", [P, C])
            n_new = sb(mid, "n_new", [P, C])
            rk2_new = sb(mid, "rk2_new", [P, C])
            cq, nk, Dk = (sb(mid, n_, [P, C]) for n_ in ("cq", "nk", "Dk"))
            QKF = sb(mid, "QKF", [P, 2, C, P])
            KB = tile4("KB")
            tot = [a] + [sb(mid, f"tot{1 << s}", [P, C, P >> s]) for s in range(1, LEVELS + 1)]
            Am = [tile4(f"Am{s}") for s in range(LEVELS)]
            Zm = [None] + [tile4(f"Zm{s}") for s in range(1, LEVELS)]
            inv, invT = tile4("inv"), tile4("invT")
            qkT = tile4("qkT")
            Vn, R, U, St, KBt = tile4("Vn"), tile4("R"), tile4("U"), tile4("St"), tile4("KBt")
            tg, z, zs, oT = tile4("tg"), tile4("z"), acc[:, 0, :, :], tile4("oT")
            zs = tile4("zs")
            hgs = sb(mid, "hgs", [P, B, P])
            ssq, w1s, w2s, lnv, rstd, fs = (sb(mid, n_, [P, C]) for n_ in ("ssq", "w1s", "w2s", "lnv", "rstd", "fs"))

            B_Q, B_K, B_L0, B_L1, B_Z, B_Y, B_S, B_O = range(8)

            def chains(i):
                return bank[i][:, :].rearrange("p (c n) -> p c n", c=C)

            def heads(ap):
                return ap.rearrange("p (b a) n -> p b a n", b=B)

            def blocks(ap, s):
                return ap.rearrange("p c (n two m) -> p c n two m", two=2, m=1 << s)

            def odd1(t_, ch, s):
                return blocks(t_[:, :, :], s)[:, ch, :, 1, :]

            def even1(t_, ch, s):
                return blocks(t_[:, :, :], s)[:, ch, :, 0, :]

            def msk(s):
                return masks[:, s, :].rearrange("p (n m) -> p n m", m=1 << s)

            wf_in, wb_in = sem("wf_in"), sem("wb_in")
            proj = [sem(f"proj_{n_}") for n_ in "qkv"]
            proj_z = sem("proj_z")
            raw_cp = [sem(f"raw_{n_}") for n_ in "qkv"]
            taps = [[sem(f"tap{j}_{n_}") for j in range(3)] for n_ in "qkv"]
            silu_raw, silu_qk, silu_v = sem("silu_raw"), sem("silu_qk"), sem("silu_v")
            silu = [silu_qk, silu_qk, silu_v]
            halo = sem("halo")
            z_in, z_clip, u_exp, r_rnd, u_minus_r, ln_w, sp_sum, sp_max, a_exp = (
                sem(n_) for n_ in ("z_in", "z_clip", "u_exp", "r_rnd", "u_minus_r", "ln_w", "sp_sum", "sp_max", "a_exp"))
            sq_q, sq_k, norms_q, norms_mm, norms_ln, norms_out = (
                sem(n_) for n_ in ("sq_q", "sq_k", "norms_q", "norms_mm", "norms_ln", "norms_out"))
            back = {}
            owner = {}

            def ev(name, who):
                back[name] = sem(name)
                owner.setdefault(who, []).append(name)
                return back[name]

            lvl0_mm = ev("lvl0_mm", "pe")
            lvl_mm = [ev(f"lvl_mm{s}", "pe") for s in range(LEVELS)]
            inv_tr = ev("inv_tr", "pe")
            z_mm = [None] + [ev(f"z_mm{s}", "pe") for s in range(1, LEVELS)]
            y_mm = [None] + [ev(f"y_mm{s}", "pe") for s in range(1, LEVELS)]
            v_tr, gate_mm, kb_tr, e_mm, w_mm, o_mm, s_mm, o_tr, wo_mm = (
                ev(n_, "pe") for n_ in ("v_tr", "gate_mm", "kb_tr", "e_mm", "w_mm", "o_mm", "s_mm", "o_tr", "wo_mm"))
            norms_in = ev("norms_in", "dve")
            qk_init = ev("qk_init", "dve")
            qk_up = [ev(f"qk_up{s}", "dve") for s in range(LEVELS)]
            lvl0_cp = ev("lvl0_cp", "dve")
            lvl_a = [ev(f"lvl_a{s}", "dve") for s in range(LEVELS)]
            lvl_q = [ev(f"lvl_q{s}", "dve") for s in range(LEVELS)]
            inv_m = [ev(f"inv_m{s}", "dve") for s in range(LEVELS)]
            v_n, r_sub, u_mul, s_up, z_gate, ssq_w, ssq_w2, f_mul, y_add = (
                ev(n_, "dve") for n_ in ("v_n", "r_sub", "u_mul", "s_up", "z_gate", "ssq_w", "ssq_w2", "f_mul", "y_add"))
            s_zero = sem("s_zero")
            hg_cp = ev("hg_cp", "pool")
            kb_init = ev("kb_init", "pool")
            kb_raw = [ev(f"kb_raw{s}", "pool") for s in range(LEVELS)]
            qk_raw = ev("qk_raw", "dve")
            kb_up = [ev(f"kb_up{s}", "pool") for s in range(LEVELS)]
            tots = [ev(f"tots{s}", "pool") for s in range(1, LEVELS + 1)]
            zs_mul = ev("zs_mul", "pool")
            gate_t = ev("gate_t", "act")
            z_cp = [None] + [ev(f"z_cp{s}", "act") for s in range(1, LEVELS)]
            kb_cp, ssq_sum, ln_v, r_std, oT_cp = (ev(n_, "act") for n_ in ("kb_cp", "ssq_sum", "ln_v", "r_std", "oT_cp"))
            zeroed = sem("zeroed")
            waited = sem("waited2")

            def step_of(i):
                return i + 1, i + 2

            def start_counts(eng, who):
                for name in owner[who]:
                    eng.sem_inc(back[name], 1)

            NFW, NBW = 8, 2
            wqkv_d = [w_.rearrange("(k p) n -> p k n", p=P) for w_ in (wq, wk, wv)]
            conv_d = [w_.rearrange("(h p) j -> p h j", p=P) for w_ in (conv_q, conv_k, conv_v)]
            dt_d = dt_bias.rearrange("(h p) -> p h", p=P)
            wo_d = wo.rearrange("(h p) n -> p h n", p=P)
            hn_v = hn[:, :, :].rearrange("p k (b s) -> p k b s", b=B)
            hfa_v = hfa[:, :].rearrange("p (b s) -> p b s", b=B)
            hga_v = hga[:, :].rearrange("p (b s) -> p b s", b=B)
            beta_v = beta[:, :, :].rearrange("p (b t) h -> p b t h", b=B)
            Y_v = Y[:, :, :].rearrange("p k (b s) -> p k b s", b=B)

            with nc.Block() as block:
                @block.sync
                def _(eng):
                    def front_weights(p):
                        cols = bass.ds(p * (PAIR * P), PAIR * P)
                        for n_ in range(3):
                            eng.dma_start(w_qkv[:, n_, :, :], wqkv_d[n_][:, :, cols]).then_inc(wf_in, 16)
                        eng.dma_start(w_fb[:, :], f_b[:, cols]).then_inc(wf_in, 16)
                        with nc.allow_non_contiguous_dma("a few scalars of each channel"):
                            for n_ in range(3):
                                eng.dma_start(cw[:, n_, :, :], conv_d[n_][:, bass.ds(p * PAIR, PAIR), :]).then_inc(wf_in, 16)
                            eng.dma_start(dtp[:, :], dt_d[:, bass.ds(p * PAIR, PAIR)]).then_inc(wf_in, 16)

                    def back_weights(p):
                        eng.dma_start(w_gb[:, :], g_b[:, bass.ds(p * (PAIR * P), PAIR * P)]).then_inc(wb_in, 16)
                        eng.dma_start(w_o[:, :, :], wo_d[:, bass.ds(p * PAIR, PAIR), :]).then_inc(wb_in, 16)

                    def front_free(p):
                        for e_ in (proj[0], proj[1], proj[2], proj_z, z_in, taps[0][2], taps[1][2], taps[2][2]):
                            eng.wait_ge(e_, p * NT)

                    front_weights(0)
                    back_weights(0)
                    with eng.Fori(1, NP) as p:
                        front_free(p)
                        front_weights(p)
                        eng.wait_ge(gate_mm, p * NT + 1)
                        eng.wait_ge(wo_mm, p * NT + 1)
                        back_weights(p)
                    front_free(NP)
                    front_weights(NP - 1)

                @block.tensor
                def _(eng):
                    def project(n_, tile, bk, waits):
                        for s_, v_ in waits:
                            eng.wait_ge(s_, v_)
                        for h in range(PAIR):
                            for k in range(KD):
                                mm = eng.matmul(heads(chains(bk))[:, :, h, :], w_qkv[:, n_, k, h * P:(h + 1) * P],
                                                hn_v[:, k, :, bass.ds(tile * P, P)], start=(k == 0), stop=(k == KD - 1))
                        mm.then_inc(proj[n_], 1)

                    def project_z(tile, now):
                        eng.wait_ge(raw_cp[1], now)
                        for h in range(PAIR):
                            mm = eng.matmul(heads(chains(B_K))[:, :, h, :], w_fb[:, h * P:(h + 1) * P],
                                            hfa_v[:, :, bass.ds(tile * P, P)], start=True, stop=True)
                        mm.then_inc(proj_z, 1)

                    def sum_squares(now, first=False):
                        eng.wait_ge(z_in, now)
                        for n_, s_ in ((0, sq_q), (1, sq_k)):
                            eng.wait_ge(s_, now)
                            for ch in range(C):
                                mm = eng.matmul(bank[B_K][:, n_ * C + ch:n_ * C + ch + 1], k2[:, ch, :], ones[:, 0:1],
                                                start=True, stop=True)
                            mm.then_inc((norms_q, norms_mm)[n_], 1)

                    def level0():
                        for ch in range(C):
                            mm = eng.matmul(chains(B_L0)[:, ch, :], ks[:, ch, :], qs[:, ch, :], start=True, stop=True)
                        mm.then_inc(lvl0_mm, 1)

                    def level(s):
                        kb = ks if s == 0 else KB
                        bk = B_L1 if s % 2 == 0 else B_L0
                        for ch in range(C):
                            mm = eng.matmul(chains(bk)[:, ch, :], kb[:, ch, :],
                                            QKF[:, :, ch, :].rearrange("p f (n two m) -> p f n two m", two=2, m=1 << s)[:, :, :, 1, :],
                                            start=True, stop=True)
                        mm.then_inc(lvl_mm[s], 1)

                    def z_product(s, now):
                        eng.wait_ge(lvl_a[s], now)
                        eng.wait_ge(inv_m[s - 1], now)
                        for ch in range(C):
                            mm = eng.matmul(bank[B_Z][:, ch * HALF:(ch + 1) * HALF], Am[s][:, ch, :], even1(inv, ch, s),
                                            start=True, stop=True)
                        mm.then_inc(z_mm[s], 1)

                    def y_product(s, now):
                        eng.wait_ge(z_cp[s], now)
                        for ch in range(C):
                            mm = eng.matmul(bank[B_Y][:, ch * HALF:(ch + 1) * HALF], Zm[s][:, ch, :], odd1(invT, ch, s),
                                            start=True, stop=True)
                        if s < LEVELS - 1:
                            for ch in range(C):
                                mm = eng.matmul(bank[B_Y][:, (C + ch) * HALF:(C + ch + 1) * HALF], invT[:, ch, :],
                                                even1(Zm[s], ch, s), start=True, stop=True)
                        mm.then_inc(y_mm[s], 1)

                    def norm_weights(n):
                        eng.wait_ge(wf_in, n)

                    start_counts(eng, "pe")
                    eng.wait_ge(zeroed, LEVELS + LEVELS - 1 + 1)
                    norm_weights(16 * NFW)
                    project(0, 0, B_Q, [])
                    project(1, 0, B_K, [])
                    project(2, 0, B_Q, [(raw_cp[0], 1)])
                    project_z(0, 1)
                    sum_squares(1, True)
                    with eng.Fori(0, N_STEPS) as i:
                        prev, now = step_of(i)
                        tile = (i + 1) % NT
                        eng.wait_ge(silu[2], prev)
                        eng.wait_ge(raw_cp[2], prev)
                        for ch in range(C):
                            mm = eng.transpose(chains(B_Q)[:, ch, :], vs[:, ch, :], ident[:, :])
                        mm.then_inc(v_tr, 1)
                        eng.wait_ge(silu[0], prev)
                        eng.wait_ge(silu[1], prev)
                        eng.wait_ge(kb_cp, prev)
                        level0()
                        eng.wait_ge(qk_init, now)
                        level(0)
                        eng.wait_ge(wf_in, ((i + 1) // NT + 1) * (16 * NFW))
                        project(0, tile, B_Q, [(v_n, now)])
                        eng.wait_ge(kb_init, now)
                        eng.wait_ge(kb_up[0], now)
                        eng.wait_ge(qk_up[0], now)
                        eng.wait_ge(lvl0_cp, now)
                        level(1)
                        project(1, tile, B_K, [(norms_ln, prev)])
                        eng.wait_ge(lvl_a[0], now)
                        for ch in range(C):
                            mm = eng.transpose(chains(B_Z)[:, ch, :], Am[0][:, ch, :], ident[:, :])
                        mm.then_inc(inv_tr, 1)
                        for s in range(2, LEVELS):
                            eng.wait_ge(kb_up[s - 1], now)
                            eng.wait_ge(qk_up[s - 1], now)
                            eng.wait_ge(lvl_q[s - 2], now)
                            level(s)
                            if s == 2:
                                project(2, tile, B_Q, [(raw_cp[0], now)])
                            if s == 3:
                                project_z(tile, now)
                            if s % 2 == 0:
                                z_product(s // 2, now)
                            else:
                                y_product(s // 2, now)
                        eng.wait_ge(hg_cp, now)
                        eng.wait_ge(y_add, prev)
                        eng.wait_ge(wb_in, (i // NT + 1) * (16 * NBW))
                        for b in range(B):
                            mm = eng.matmul(bank[B_O][:, b * PAIR * P:(b + 1) * PAIR * P], hgs[:, b, :], w_gb[:, :],
                                            start=True, stop=True)
                        mm.then_inc(gate_mm, 1)
                        eng.wait_ge(qk_up[LEVELS - 1], now)
                        eng.wait_ge(s_up, prev)
                        eng.wait_ge(s_zero, i // NT + 1)
                        for ch in range(C):
                            mm = eng.matmul(chains(B_S)[:, ch, :], QKF[:, 1, ch, :], St[:, ch, :], start=True, stop=True)
                        mm.then_inc(e_mm, 1)
                        eng.wait_ge(kb_up[LEVELS - 1], now)
                        eng.wait_ge(lvl_q[LEVELS - 2], now)
                        for ch in range(C):
                            mm = eng.transpose(chains(B_L0)[:, ch, :], KB[:, ch, :], ident[:, :])
                        mm.then_inc(kb_tr, 1)
                        y_product(3, now)
                        for s in range(4, LEVELS):
                            z_product(s, now)
                            if s == 4:
                                sum_squares(now)
                            y_product(s, now)
                        eng.wait_ge(inv_m[LEVELS - 1], now)
                        eng.wait_ge(r_sub, now)
                        for ch in range(C):
                            mm = eng.matmul(chains(B_S)[:, ch, :], invT[:, ch, :], R[:, ch, :], start=True, stop=True)
                        mm.then_inc(w_mm, 1)
                        eng.wait_ge(u_mul, now)
                        eng.wait_ge(lvl_q[LEVELS - 1], now)
                        eng.wait_ge(gate_t, now)
                        for ch in range(C):
                            eng.matmul(chains(B_O)[:, ch, :], QKF[:, 0, ch, :], St[:, ch, :], start=True, stop=False)
                            mm = eng.matmul(chains(B_O)[:, ch, :], qkT[:, ch, :], U[:, ch, :], start=False, stop=True)
                        mm.then_inc(o_mm, 1)
                        eng.wait_ge(kb_cp, now)
                        for ch in range(C):
                            mm = eng.matmul(chains(B_S)[:, ch, :], KBt[:, ch, :], U[:, ch, :], start=True, stop=True)
                        mm.then_inc(s_mm, 1)
                        eng.wait_ge(zs_mul, now)
                        for ch in range(C):
                            mm = eng.transpose(chains(B_O)[:, ch, :], zs[:, ch, :], ident[:, :])
                        mm.then_inc(o_tr, 1)
                        eng.wait_ge(oT_cp, now)
                        for k in range(KD):
                            for h in range(PAIR):
                                mm = eng.matmul(bank[B_O][:, k * B * P:(k + 1) * B * P], w_o[:, h, k * P:(k + 1) * P],
                                                heads(oT[:, :, :])[:, :, h, :], start=(h == 0), stop=(h == PAIR - 1))
                        mm.then_inc(wo_mm, 1)

                @block.scalar
                def _(eng):
                    def take_raw(n_, bk, now, first=False):
                        eng.wait_ge(proj[n_], now)
                        eng.wait_ge(halo, now)
                        eng.activation(raw[:, n_, :, KS - 1:], chains(bk), ACT.Copy)
                        for h in range(PAIR):
                            x_ = eng.activation(heads(acc[:, n_, :, :])[:, :, h, :], heads(chains(bk))[:, :, h, :], ACT.Copy,
                                                scale=cw[:, n_, h, KS - 1:KS])
                        x_.then_inc(raw_cp[n_], 1)

                    def take_z(now):
                        eng.wait_ge(proj_z, now)
                        for h in range(PAIR):
                            x_ = eng.activation(heads(zp[:, :, :])[:, :, h, :], heads(chains(B_K))[:, :, h, :], ACT.Identity,
                                                bias=dtp[:, h:h + 1])
                        x_.then_inc(z_in, 1)

                    def silus(now):
                        for e_ in (lvl_mm[0], qk_init, kb_up[0], kb_init, v_tr):
                            eng.wait_ge(e_, now)
                        eng.wait_ge(taps[0][2], now)
                        eng.wait_ge(taps[1][2], now)
                        eng.activation(acc[:, 0:2, :, :], acc[:, 0:2, :, :], ACT.Silu).then_inc(silu_raw, 1)
                        eng.wait_ge(taps[2][2], now)
                        eng.activation(vs[:, :, :], acc[:, 2, :, :], ACT.Silu).then_inc(silu_v, 1)
                        eng.wait_ge(silu_raw, now)
                        eng.activation(qk[:, :, :, :], acc[:, 0:2, :, :], ACT.Copy, scale=QK_SCALE).then_inc(silu_qk, 1)

                    def softplus_logs(now):
                        eng.preload_act_table_set(LN_EXP)
                        eng.wait_ge(z_clip, now)
                        eng.activation(u[:, :, :], zc[:, :, :], ACT.Exp).then_inc(u_exp, 1)
                        eng.wait_ge(u_exp, now)
                        eng.activation(lnw[:, :, :], u[:, :, :], ACT.Ln, bias=1.0).then_inc(ln_w, 1)

                    def decays(pair, now):
                        eng.wait_ge(sp_max, now)
                        for e_ in (qk_up[0], kb_up[0], tots[0]):
                            eng.wait_ge(e_, now)
                        for h in range(PAIR):
                            x_ = eng.activation(heads(a[:, :, :])[:, :, h, :], heads(r[:, :, :])[:, :, h, :], ACT.Exp,
                                                scale=negA[:, bass.ds(pair * PAIR + h, 1)])
                        x_.then_inc(a_exp, 1)

                    def norms(now):
                        eng.wait_ge(norms_mm, now)
                        eng.activation(lns[:, :], bank[B_K][:, 0:2 * C], ACT.Ln, bias=eps6[:, :],
                                       scale=QK_SCALE ** -2).then_inc(norms_ln, 1)
                        eng.wait_ge(norms_ln, now)
                        eng.wait_ge(norms_in, now)
                        eng.activation(cq_new[:, :], lns[:, 0:C], ACT.Exp, scale=-0.5, bias=qscale[:, :])
                        eng.activation(n_new[:, :], lns[:, C:], ACT.Exp, scale=0.5)
                        eng.activation(rk2_new[:, :], lns[:, C:], ACT.Exp, scale=-1.0).then_inc(norms_out, 1)

                    start_counts(eng, "act")
                    eng.wait_ge(wf_in, 16 * NFW)
                    take_raw(0, B_Q, 1)
                    take_raw(1, B_K, 1)
                    take_raw(2, B_Q, 1)
                    take_z(1)
                    silus(1)
                    softplus_logs(1)
                    norms(1)
                    decays(0, 1)
                    with eng.Fori(0, N_STEPS) as i:
                        prev, now = step_of(i)
                        eng.wait_ge(wf_in, ((i + 1) // NT + 1) * (16 * NFW))
                        take_raw(0, B_Q, now)
                        take_raw(1, B_K, now)

                        def take_zm(s):
                            eng.wait_ge(z_mm[s], now)
                            eng.activation(blocks(Zm[s][:, :, :], s)[:, :, :, 0, :],
                                           bank[B_Z][:, 0:C * HALF].rearrange("p (c n m) -> p c n m", c=C, m=1 << s),
                                           ACT.Copy).then_inc(z_cp[s], 1)

                        take_raw(2, B_Q, now)
                        take_zm(1)
                        take_z(now)
                        take_zm(2)
                        take_zm(3)
                        eng.wait_ge(kb_tr, now)
                        eng.activation(KBt[:, :, :], chains(B_L0), ACT.Copy).then_inc(kb_cp, 1)
                        eng.wait_ge(gate_mm, now)
                        eng.activation(tg[:, :, :], chains(B_O), ACT.Tanh, scale=0.5).then_inc(gate_t, 1)
                        silus(now)
                        take_zm(4)
                        softplus_logs(now)
                        take_zm(5)
                        norms(now)
                        take_zm(6)
                        decays(((i + 1) // NT) % NP, now)
                        eng.wait_ge(z_gate, now)
                        for ch in range(C):
                            x_ = eng.activation(oT[:, ch, :], z[:, ch, :], ACT.Square, scale=QK_SCALE ** -2, accum_out=ssq[:, ch:ch + 1])
                        x_.then_inc(ssq_sum, 1)
                        eng.wait_ge(ssq_w2, now)
                        eng.activation(lnv[:, :], w2s[:, :], ACT.Ln, bias=eps6[:, :], scale=1.0 / P).then_inc(ln_v, 1)
                        eng.wait_ge(ln_v, now)
                        eng.activation(rstd[:, :], lnv[:, :], ACT.Exp, scale=-0.5).then_inc(r_std, 1)
                        eng.wait_ge(o_tr, now)
                        eng.activation(oT[:, :, :], chains(B_O), ACT.Copy, scale=onw[:, :]).then_inc(oT_cp, 1)

                @block.gpsimd
                def _(eng):
                    def squares(now):
                        eng.wait_ge(silu[0], now)
                        eng.tensor_tensor(k2[:, :, :], qs[:, :, :], qs[:, :, :], ALU.mult).then_inc(sq_q, 1)
                        eng.wait_ge(silu[1], now)
                        eng.wait_ge(norms_q, now)
                        eng.tensor_tensor(k2[:, :, :], ks[:, :, :], ks[:, :, :], ALU.mult).then_inc(sq_k, 1)

                    def softplus_low(now):
                        eng.wait_ge(r_rnd, now)
                        eng.wait_ge(ln_w, now)
                        eng.tensor_tensor(u[:, :, :], u[:, :, :], r[:, :, :], ALU.subtract).then_inc(u_minus_r, 1)
                        eng.wait_ge(u_minus_r, now)
                        eng.tensor_tensor(r[:, :, :], lnw[:, :, :], u[:, :, :], ALU.add).then_inc(sp_sum, 1)

                    def round_off(ap, done):
                        eng.tensor_scalar(ap, ap, ROUND, -ROUND, ALU.add, ALU.add).then_inc(done, 1)

                    start_counts(eng, "pool")
                    for s in range(LEVELS):
                        eng.memset(Am[s][:, :, :], 0.0).then_inc(zeroed, 1)
                    for s in range(1, LEVELS):
                        eng.memset(Zm[s][:, :, :], 0.0).then_inc(zeroed, 1)
                    eng.memset(raw[:, :, :, :], 0.0).then_inc(zeroed, 1)
                    squares(1)
                    softplus_low(1)
                    with eng.Fori(0, N_STEPS) as i:
                        prev, now = step_of(i)
                        tile = i % NT
                        for e_ in (silu[1], a_exp, kb_tr):
                            eng.wait_ge(e_, prev)
                        eng.tensor_tensor(blocks(KB[:, :, :], 0)[:, :, :, 0, 0], blocks(ks[:, :, :], 0)[:, :, :, 0, 0],
                                          blocks(a[:, :, :], 0)[:, :, :, 1, 0], ALU.mult).then_inc(kb_raw[0], 1)
                        eng.tensor_copy(blocks(KB[:, :, :], 0)[:, :, :, 1, :], blocks(ks[:, :, :], 0)[:, :, :, 1, :]).then_inc(kb_init, 1)
                        eng.wait_ge(kb_raw[0], now)
                        eng.sem_inc(waited, 1)
                        round_off(blocks(KB[:, :, :], 0)[:, :, :, 0, :], kb_up[0])
                        eng.wait_ge(s_up, prev)
                        for s in range(LEVELS):
                            src = tot[s][:, :, :].rearrange("p c (n two) -> p c n two", two=2)
                            if s:
                                eng.wait_ge(tots[s - 1], now)
                            eng.tensor_tensor(tot[s + 1][:, :, :], src[:, :, :, 0], src[:, :, :, 1], ALU.mult).then_inc(tots[s], 1)
                        eng.wait_ge(gate_mm, prev)
                        eng.tensor_copy(hgs[:, :, :], hga_v[:, :, bass.ds(tile * P, P)]).then_inc(hg_cp, 1)
                        for s in range(1, LEVELS):
                            m = 1 << s
                            eng.wait_ge(lvl_mm[s], now)
                            eng.wait_ge(kb_up[s - 1], now)
                            if s == 1:
                                eng.wait_ge(kb_init, now)
                            t_ = tot[s][:, :, :].rearrange("p c (n two) -> p c n two", two=2)[:, :, :, 1:2]
                            e_ = blocks(KB[:, :, :], s)[:, :, :, 0, :]
                            eng.tensor_tensor(e_, e_, t_.to_broadcast([P, C, P // (2 * m), m]), ALU.mult).then_inc(kb_raw[s], 1)
                            eng.wait_ge(kb_raw[s], now)
                            eng.sem_inc(waited, 1)
                            round_off(e_, kb_up[s])
                        squares(now)
                        softplus_low(now)
                        eng.wait_ge(f_mul, now)
                        eng.tensor_tensor(zs[:, :, :], z[:, :, :], fs[:, :].unsqueeze(2).to_broadcast([P, C, P]),
                                          ALU.mult).then_inc(zs_mul, 1)

                @block.vector
                def _(eng):
                    def tap(n_, j, now):
                        for h in range(PAIR):
                            dst = heads(acc[:, n_, :, :])[:, :, h, :]
                            x_ = eng.scalar_tensor_tensor(dst, heads(raw[:, n_, :, :])[:, :, h, KS - 2 - j:KS - 2 - j + P],
                                                          cw[:, n_, h, KS - 2 - j:KS - 1 - j], dst, ALU.mult, ALU.add)
                        x_.then_inc(taps[n_][j], 1)

                    def conv(n_, now):
                        eng.wait_ge(raw_cp[n_], now)
                        for j in range(3):
                            if j:
                                eng.wait_ge(taps[n_][j - 1], now)
                            tap(n_, j, now)

                    def next_halo(keep, now):
                        eng.wait_ge(taps[2][2], now)
                        eng.tensor_scalar(raw[:, :, :, 0:KS - 1], raw[:, :, :, P:], keep, None, ALU.mult).then_inc(halo, 1)

                    def clip_z(now):
                        eng.wait_ge(z_in, now)
                        eng.tensor_scalar(zc[:, :, :], zp[:, :, :], SOFTPLUS_MAX, None, ALU.min).then_inc(z_clip, 1)

                    def round_w(now):
                        eng.wait_ge(u_exp, now)
                        eng.tensor_scalar(r[:, :, :], u[:, :, :], 1.0, -1.0, ALU.add, ALU.add).then_inc(r_rnd, 1)

                    def softplus_max(now):
                        eng.wait_ge(sp_sum, now)
                        eng.tensor_tensor(r[:, :, :], r[:, :, :], zp[:, :, :], ALU.max).then_inc(sp_max, 1)

                    def level_products(s, now):
                        bk = B_L1 if s % 2 == 0 else B_L0
                        m = 1 << s
                        eng.wait_ge(lvl_q[s - 1] if s else lvl0_cp, now)
                        ps = chains(bk).rearrange("p c (f n m) -> p c f n m", f=2, m=m)
                        for ch in range(C):
                            x_ = eng.scalar_tensor_tensor(odd1(Am[s], ch, s), ps[:, ch, 1, :, :], Dk[:, ch:ch + 1], msk(s),
                                                          ALU.mult, ALU.mult)
                        x_.then_inc(lvl_a[s], 1)
                        for ch in range(C):
                            x_ = eng.copy_predicated(odd1(qkT, ch, s), msk(s).bitcast(I32), ps[:, ch, 0, :, :])
                        x_.then_inc(lvl_q[s], 1)

                    def grow_f(s, now):
                        m = 1 << s
                        eng.wait_ge(lvl_mm[s], now)
                        if s:
                            eng.wait_ge(tots[s - 1], now)
                            eng.wait_ge(qk_up[s - 1], now)
                        else:
                            eng.wait_ge(qk_init, now)
                        t_ = tot[s][:, :, :].rearrange("p c (n two) -> p c n two", two=2)[:, :, :, 0:1]
                        for f in range(2):
                            o_ = blocks(QKF[:, f, :, :], s)[:, :, :, 1, :]
                            x_ = eng.tensor_tensor(o_, o_, t_.to_broadcast([P, C, P // (2 * m), m]), ALU.mult)
                        x_.then_inc(qk_raw, 1)
                        eng.wait_ge(qk_raw, (now - 2) * (LEVELS + 1) + s + 3)
                        o_ = QKF[:, :, :, :].rearrange("p f c n -> p (f c) n").rearrange("p c (n two m) -> p c n two m", two=2, m=m)[:, :, :, 1, :]
                        eng.tensor_scalar(o_, o_, ROUND, -ROUND, ALU.add, ALU.add).then_inc(qk_up[s], 1)

                    def grow_inverse(s, now):
                        eng.wait_ge(y_mm[s], now)
                        eng.wait_ge(inv_m[s - 1], now)
                        m = 1 << s
                        ps = bank[B_Y][:, :].rearrange("p (f c n m) -> p f c n m", f=2, c=C, m=m)
                        o_ = blocks(invT[:, :, :], s)[:, :, :, 1, :]
                        x_ = eng.tensor_tensor(o_, o_, ps[:, 0, :, :, :], ALU.subtract)
                        if s < LEVELS - 1:
                            e_ = blocks(inv[:, :, :], s)[:, :, :, 0, :]
                            x_ = eng.tensor_tensor(e_, e_, ps[:, 1, :, :, :], ALU.subtract)
                        x_.then_inc(inv_m[s], 1)

                    identb = ident[:, :].unsqueeze(1).to_broadcast([P, C, P])
                    start_counts(eng, "dve")
                    eng.wait_ge(zeroed, 2 * LEVELS)
                    eng.sem_inc(halo, 1)
                    eng.wait_ge(wf_in, 16 * NFW)
                    for n_ in range(3):
                        conv(n_, 1)
                    next_halo(1.0, 1)
                    clip_z(1)
                    round_w(1)
                    softplus_max(1)
                    with eng.Fori(0, NP) as pair:
                        eng.memset(St[:, :, :], 0.0).then_inc(s_zero, 1)
                        with eng.Fori(0, NT) as t:
                            i = pair * NT + t
                            prev, now = step_of(i)
                            eng.wait_ge(norms_out, prev)
                            eng.tensor_copy(cq[:, :], cq_new[:, :])
                            eng.tensor_scalar(nk[:, :], n_new[:, :], QK_SCALE ** 2, None, ALU.mult)
                            eng.scalar_tensor_tensor(Dk[:, :].rearrange("p (b a) -> p b a", b=B),
                                              rk2_new[:, :].rearrange("p (b a) -> p b a", b=B), QK_SCALE ** -2,
                                              beta_v[:, :, bass.ds(t, 1), bass.ds(pair * PAIR, PAIR)].rearrange("p b o a -> p b (o a)"),
                                              ALU.mult, ALU.mult).then_inc(norms_in, 1)
                            eng.wait_ge(a_exp, prev)
                            for f, t_ in ((0, qs), (1, ks)):
                                x_ = eng.tensor_tensor(QKF[:, f, :, :], t_[:, :, :], a[:, :, :], ALU.mult)
                            x_.then_inc(qk_raw, 1)
                            eng.wait_ge(qk_raw, i * (LEVELS + 1) + 2)
                            eng.tensor_scalar(QKF[:, :, :, :], QKF[:, :, :, :], ROUND, -ROUND, ALU.add, ALU.add).then_inc(qk_init, 1)
                            eng.wait_ge(norms_in, now)
                            eng.wait_ge(v_tr, now)
                            eng.tensor_tensor(Vn[:, :, :], chains(B_Q), nk[:, :].unsqueeze(2).to_broadcast([P, C, P]),
                                              ALU.mult).then_inc(v_n, 1)
                            grow_f(0, now)
                            eng.wait_ge(lvl0_mm, now)
                            eng.tensor_tensor(qkT[:, :, :], chains(B_L0), identb, ALU.mult).then_inc(lvl0_cp, 1)
                            level_products(0, now)
                            grow_f(1, now)
                            level_products(1, now)
                            eng.tensor_tensor(invT[:, :, :], identb, Am[0][:, :, :], ALU.subtract)
                            eng.wait_ge(inv_tr, now)
                            eng.tensor_tensor(inv[:, :, :], identb, chains(B_Z), ALU.subtract).then_inc(inv_m[0], 1)
                            conv(0, now)
                            grow_f(2, now)
                            level_products(2, now)
                            conv(1, now)
                            grow_f(3, now)
                            level_products(3, now)
                            grow_inverse(1, now)
                            conv(2, now)
                            grow_f(4, now)
                            level_products(4, now)
                            next_halo(keep[:, bass.ds(t, 1)], now)
                            clip_z(now)
                            grow_f(5, now)
                            level_products(5, now)
                            grow_inverse(2, now)
                            grow_f(6, now)
                            level_products(6, now)
                            grow_inverse(3, now)
                            eng.wait_ge(e_mm, now)
                            eng.wait_ge(v_n, now)
                            eng.tensor_tensor(R[:, :, :], Vn[:, :, :], chains(B_S), ALU.subtract).then_inc(r_sub, 1)
                            grow_inverse(4, now)
                            round_w(now)
                            grow_inverse(5, now)
                            softplus_max(now)
                            grow_inverse(6, now)
                            eng.wait_ge(w_mm, now)
                            eng.tensor_tensor(U[:, :, :], chains(B_S), Dk[:, :].unsqueeze(2).to_broadcast([P, C, P]),
                                              ALU.mult).then_inc(u_mul, 1)
                            eng.tensor_tensor(w1s[:, :], cq[:, :], cq[:, :], ALU.mult).then_inc(ssq_w, 1)
                            eng.wait_ge(o_mm, now)
                            eng.scalar_tensor_tensor(z[:, :, :], tg[:, :, :], 1.0, chains(B_O), ALU.add, ALU.mult).then_inc(z_gate, 1)
                            eng.wait_ge(s_mm, now)
                            eng.wait_ge(tots[LEVELS - 1], now)
                            for ch in range(C):
                                x_ = eng.scalar_tensor_tensor(St[:, ch, :], St[:, ch, :], tot[LEVELS][:, ch, :], chains(B_S)[:, ch, :],
                                                              ALU.mult, ALU.add)
                            x_.then_inc(s_up, 1)
                            eng.wait_ge(ssq_sum, now)
                            eng.wait_ge(ssq_w, now)
                            eng.tensor_tensor(w2s[:, :], ssq[:, :], w1s[:, :], ALU.mult).then_inc(ssq_w2, 1)
                            eng.wait_ge(r_std, now)
                            eng.scalar_tensor_tensor(fs[:, :], cq[:, :], QK_SCALE ** -2, rstd[:, :], ALU.mult, ALU.mult).then_inc(f_mul, 1)
                            eng.wait_ge(wo_mm, now)
                            y_ = Y_v[:, :, :, bass.ds(t * P, P)]
                            eng.tensor_tensor(y_, y_, bank[B_O][:, :].rearrange("p (k b n) -> p k b n", k=KD, b=B),
                                              ALU.add).then_inc(y_add, 1)
                            eng.wait_ge(s_up, now)

        end_phase()

        with ExitStack() as ph:
            xt = sb(ph, "xt", [P, SUB, D])
            w1_s, w3_s = sb(ph, "w1_s", [P, KD, FF]), sb(ph, "w3_s", [P, KD, FF])
            w2_s = sb(ph, "w2_s", [P, FT, D])
            W1T, W3T = sb(ph, "W1T", [P, KD, FF]), sb(ph, "W3T", [P, KD, FF])
            W2T = sb(ph, "W2T", [P, FT, D])
            W1n, W3n = sb(ph, "W1n", [P, FT, D]), sb(ph, "W3n", [P, FT, D])
            W2n = [sb(ph, f"W2n{i}", [P, KD, FF]) for i in range(2)]
            n2 = sb(ph, "n2", [P, KD])
            def tile2(name):
                return sb(ph, name, [P, KD, GROUP])
            sq, h2, ao, x3, dev, h3, x4 = (tile2(n_) for n_ in ("sq3", "h2", "ao", "x3", "dev", "h3", "x4"))
            rr = sb(ph, "rr3", [P, GROUP])
            sg = sb(ph, "sg", [P, 2, GROUP])
            G = sb(ph, "G", [P, FT, GROUP])
            ot = sb(ph, "ot", [P, SUB, D])

            ld_w, ld_x, st_o = sem("ld_w3"), sem("ld_x3"), sem("st_out")
            had, w_tr, w_cp = sem("had"), sem("w_tr"), sem("w_cp")
            sq1, sum1, ln1, rs1, h2_ok = (sem(n_) for n_ in ("sq1", "sum1", "ln1", "rs1", "h2_ok"))
            up, act_ok, g_ok, down = ([sem(f"{n_}{j}") for j in range(2)] for n_ in ("up", "silu_ok", "g_ok", "down"))
            ao_ok, xT_mm, x3_ok, sum2, dev_ok, sq2, sum3, ln2, rs2, nrm_ok, h3_ok, x4_ok, oT_mm, ot_ok = (
                sem(n_) for n_ in ("ao_ok", "xT_mm", "x3_ok", "sum2", "dev_ok", "sq2", "sum3", "ln2", "rs2", "nrm_ok",
                                   "h3_ok", "x4_ok", "oT_mm", "ot_ok"))
            N_HAD = FF.bit_length() - 1
            out_v = out.rearrange("b (g s p) d -> (b g) p s d", s=SUB, p=P)
            x_v = x.rearrange("b (g s p) d -> (b g) p s d", s=SUB, p=P)

            with nc.Block() as block:
                @block.sync
                def _(eng):
                    for s_, d_ in ((w1_s, w1), (w3_s, w3)):
                        eng.dma_start(s_[:, :, :], d_.rearrange("(k p) n -> p k n", p=P)).then_inc(ld_w, 16)
                    for s_, d_ in ((w2_s, w2), (W1n, W1), (W3n, W3)):
                        eng.dma_start(s_[:, :, :], d_.rearrange("(f p) n -> p f n", p=P)).then_inc(ld_w, 16)
                    eng.dma_start(W2n[0][:, :, :], W2.rearrange("(k p) n -> p k n", p=P)).then_inc(ld_w, 16)
                    with nc.allow_non_contiguous_dma("a vector, once"):
                        eng.dma_start(n2[:, :], norm2_w.rearrange("(k p) -> p k", p=P)).then_inc(ld_w, 16)
                    eng.dma_start(xt[:, :, :], x_v[0]).then_inc(ld_x, 16)
                    with eng.Fori(0, NG) as g:
                        eng.wait_ge(ot_ok, g + 1)
                        eng.dma_start(out_v[bass.ds(g, 1)].rearrange("o p s d -> p (o s) d"), ot[:, :, :]).then_inc(st_o, 16)
                        eng.wait_ge(xT_mm, g + 1)
                        eng.dma_start(xt[:, :, :], x_v[bass.ds((g + 1) % NG, 1)].rearrange("o p s d -> p (o s) d")).then_inc(ld_x, 16)
                    eng.wait_ge(st_o, 16 * NG)
                    eng.wait_ge(ld_x, 16 * (NG + 1))

                @block.tensor
                def _(eng):
                    eng.wait_ge(ld_w, 16 * 7)
                    n = 0
                    for src, dst in ((W1n, W1T), (W3n, W3T)):
                        for k in range(KD):
                            for q_ in range(FT // 4):
                                if n >= 4:
                                    eng.wait_ge(w_cp, n - 3)
                                for f in range(4):
                                    mm = eng.transpose(bank[n % 4][:, f * P:(f + 1) * P], src[:, q_ * 4 + f, k * P:(k + 1) * P], ident[:, :])
                                mm.then_inc(w_tr, 1)
                                n += 1
                    eng.wait_ge(had, 2 * N_HAD)
                    Wh = W2n[N_HAD % 2]
                    for f2 in range(FT // 2):
                        eng.wait_ge(w_cp, n - 3)
                        for f in range(2):
                            for k in range(KD):
                                mm = eng.transpose(bank[n % 4][:, (f * KD + k) * P:(f * KD + k + 1) * P],
                                                   Wh[:, k, (f2 * 2 + f) * P:(f2 * 2 + f + 1) * P], ident[:, :])
                        mm.then_inc(w_tr, 1)
                        n += 1
                    eng.wait_ge(w_cp, n)

                    def feed_forward(j, wa, wb, wd, src, g):
                        for f in range(FT):
                            eng.wait_ge(g_ok[j], g * FT + f - 1) if f >= 2 else None
                            for bk, w_ in ((f % 2, wa), (2 + f % 2, wb)):
                                for k in range(KD):
                                    mm = eng.matmul(bank[bk][:, :], w_[:, k, f * P:(f + 1) * P], src[:, k, :],
                                                    start=(k == 0), stop=(k == KD - 1))
                            mm.then_inc(up[j], 1)
                        eng.wait_ge(g_ok[j], (g + 1) * FT)
                        for k in range(KD):
                            for f in range(FT):
                                mm = eng.matmul(bank[4 + k][:, :], wd[:, f, k * P:(k + 1) * P], G[:, f, :],
                                                start=(f == 0), stop=(f == FT - 1))
                        mm.then_inc(down[j], 1)

                    with eng.Fori(0, NG) as g:
                        eng.wait_ge(sq1, g + 1)
                        for k in range(KD):
                            mm = eng.matmul(bank[2][:, :], ones[:, :], sq[:, k, :], start=(k == 0), stop=(k == KD - 1))
                        mm.then_inc(sum1, 1)
                        eng.wait_ge(ld_x, 16 * (g + 1))
                        for k in range(KD):
                            for s in range(SUB):
                                mm = eng.transpose(bank[6 + k][:, s * P:(s + 1) * P], xt[:, s, k * P:(k + 1) * P], ident[:, :])
                        mm.then_inc(xT_mm, 1)
                        eng.wait_ge(h2_ok, g + 1)
                        feed_forward(0, w1_s, w3_s, w2_s, h2, g)
                        eng.wait_ge(x3_ok, g + 1)
                        for k in range(KD):
                            mm = eng.matmul(bank[2][:, :], ones[:, :], x3[:, k, :], start=(k == 0), stop=(k == KD - 1))
                        mm.then_inc(sum2, 1)
                        eng.wait_ge(sq2, g + 1)
                        for k in range(KD):
                            mm = eng.matmul(bank[3][:, :], ones[:, :], sq[:, k, :], start=(k == 0), stop=(k == KD - 1))
                        mm.then_inc(sum3, 1)
                        eng.wait_ge(h3_ok, g + 1)
                        feed_forward(1, W1T, W3T, W2T, h3, g)
                        eng.wait_ge(x4_ok, g + 1)
                        for k in range(KD):
                            for s in range(SUB):
                                mm = eng.transpose(bank[6 + k][:, s * P:(s + 1) * P], x4[:, k, s * P:(s + 1) * P], ident[:, :])
                        mm.then_inc(oT_mm, 1)
                        eng.wait_ge(ot_ok, g + 1)

                @block.scalar
                def _(eng):
                    def silu_up(j, g):
                        for f in range(FT):
                            eng.wait_ge(up[j], g * FT + f + 1)
                            if f >= 2:
                                eng.wait_ge(g_ok[j], g * FT + f - 1)
                            eng.activation(sg[:, f % 2, :], bank[f % 2][:, :], ACT.Silu).then_inc(act_ok[j], 1)

                    with eng.Fori(0, NG) as g:
                        tok = bass.ds(g * GROUP, GROUP)
                        half = bass.ds(g // GB, 1)
                        eng.activation(sq[:, :, :], Y[:, :, tok], ACT.Square).then_inc(sq1, 1)
                        eng.preload_act_table_set(LN_EXP)
                        eng.wait_ge(sum1, g + 1)
                        eng.activation(rr[:, :], bank[2][:, :], ACT.Ln, bias=eps6[:, :], scale=1.0 / D).then_inc(ln1, 1)
                        eng.wait_ge(ln1, g + 1)
                        eng.activation(rr[:, :], rr[:, :], ACT.Exp, scale=-0.5).then_inc(rs1, 1)
                        silu_up(0, g)
                        eng.wait_ge(dev_ok, g + 1)
                        eng.activation(sq[:, :, :], dev[:, :, :], ACT.Square).then_inc(sq2, 1)
                        eng.preload_act_table_set(LN_EXP)
                        eng.wait_ge(sum3, g + 1)
                        eng.activation(rr[:, :], bank[3][:, :], ACT.Ln, bias=eps5[:, :], scale=1.0 / D).then_inc(ln2, 1)
                        eng.wait_ge(ln2, g + 1)
                        eng.activation(rr[:, :], rr[:, :], ACT.Exp, scale=-0.5).then_inc(rs2, 1)
                        eng.wait_ge(nrm_ok, g + 1)
                        for k in range(KD):
                            x_ = eng.activation(h3[:, k, :], dev[:, k, :], ACT.Identity,
                                                bias=modv[:, SB_, k, half], scale=modv[:, CB, k, half])
                        x_.then_inc(h3_ok, 1)
                        silu_up(1, g)
                        eng.wait_ge(oT_mm, g + 1)
                        eng.wait_ge(st_o, 16 * g) if False else None
                        for k in range(KD):
                            x_ = eng.activation(ot[:, :, k * P:(k + 1) * P], bank[6 + k][:, :].rearrange("p (s n) -> p s n", n=P), ACT.Copy)
                        x_.then_inc(ot_ok, 1)

                @block.vector
                def _(eng):
                    eng.wait_ge(ld_w, 16 * 7)
                    for j in range(N_HAD):
                        src, dst = (W2n[j % 2], W2n[(j + 1) % 2])
                        sv, dv = (t_[:, :, :].rearrange("p k (n two m) -> p (k n) two m", two=2, m=1 << j) for t_ in (src, dst))
                        if j:
                            eng.wait_ge(had, 2 * j)
                        eng.tensor_tensor(dv[:, :, 0, :], sv[:, :, 0, :], sv[:, :, 1, :], ALU.add).then_inc(had, 1)
                        eng.tensor_tensor(dv[:, :, 1, :], sv[:, :, 0, :], sv[:, :, 1, :], ALU.subtract).then_inc(had, 1)
                    n = 0
                    for dst in (W1T, W3T):
                        for k in range(KD):
                            for q_ in range(FT // 4):
                                eng.wait_ge(w_tr, n + 1)
                                eng.tensor_copy(dst[:, k, q_ * 512:(q_ + 1) * 512], bank[n % 4][:, :]).then_inc(w_cp, 1)
                                n += 1
                    for f2 in range(FT // 2):
                        eng.wait_ge(w_tr, n + 1)
                        eng.tensor_scalar(W2T[:, f2 * 2:f2 * 2 + 2, :], bank[n % 4][:, :].rearrange("p (f n) -> p f n", f=2),
                                          float(FF) ** -0.5, None, ALU.mult).then_inc(w_cp, 1)
                        n += 1

                    def gate_up(j, g):
                        for f in range(FT):
                            eng.wait_ge(act_ok[j], g * FT + f + 1)
                            eng.tensor_tensor(G[:, f, :], sg[:, f % 2, :], bank[2 + f % 2][:, :], ALU.mult).then_inc(g_ok[j], 1)

                    with eng.Fori(0, NG) as g:
                        tok = bass.ds(g * GROUP, GROUP)
                        half = bass.ds(g // GB, 1)
                        eng.wait_ge(rs1, g + 1)
                        for k in range(KD):
                            x_ = eng.scalar_tensor_tensor(h2[:, k, :], Y[:, k, tok], n2[:, k:k + 1], rr[:, :], ALU.mult, ALU.mult)
                        x_.then_inc(h2_ok, 1)
                        gate_up(0, g)
                        eng.wait_ge(down[0], g + 1)
                        for k in range(KD):
                            x_ = eng.tensor_tensor(ao[:, k, :], Y[:, k, tok], bank[4 + k][:, :], ALU.add)
                        x_.then_inc(ao_ok, 1)
                        eng.wait_ge(ao_ok, g + 1)
                        eng.wait_ge(xT_mm, g + 1)
                        for k in range(KD):
                            x_ = eng.scalar_tensor_tensor(x3[:, k, :], ao[:, k, :], modv[:, GA, k, half], bank[6 + k][:, :],
                                                          ALU.mult, ALU.add)
                        x_.then_inc(x3_ok, 1)
                        eng.wait_ge(x3_ok, g + 1)
                        eng.wait_ge(sum2, g + 1)
                        for k in range(KD):
                            x_ = eng.scalar_tensor_tensor(dev[:, k, :], bank[2][:, :], -1.0 / D, x3[:, k, :], ALU.mult, ALU.add)
                        x_.then_inc(dev_ok, 1)
                        eng.wait_ge(dev_ok, g + 1)
                        eng.wait_ge(rs2, g + 1)
                        for k in range(KD):
                            x_ = eng.tensor_tensor(dev[:, k, :], dev[:, k, :], rr[:, :], ALU.mult)
                        x_.then_inc(nrm_ok, 1)
                        gate_up(1, g)
                        eng.wait_ge(down[1], g + 1)
                        for k in range(KD):
                            x_ = eng.scalar_tensor_tensor(x4[:, k, :], bank[4 + k][:, :], modv[:, GBv, k, half], x3[:, k, :],
                                                          ALU.mult, ALU.add)
                        x_.then_inc(x4_ok, 1)


_INS = ["L0_attn_x", "L0_attn_norm1_w", "L0_attn_wq", "L0_attn_wk", "L0_attn_wv", "L0_attn_conv_q", "L0_attn_conv_k",
        "L0_attn_conv_v", "L0_attn_f_a", "L0_attn_f_b", "L0_attn_A_log", "L0_attn_dt_bias", "L0_attn_b_w",
        "L0_attn_g_a", "L0_attn_g_b", "L0_attn_onorm_w", "L0_attn_wo", "L0_attn_norm2_w", "L0_attn_w1", "L0_attn_w2",
        "L0_attn_w3", "L0_ffn_W1", "L0_ffn_W2", "L0_ffn_W3", "L0_c", "L0_wmod"]


def constants(n_tiles):
    import numpy as np

    j = np.arange(P)[:, None]
    parts = [np.eye(P)]
    for s in range(LEVELS):
        m = 1 << s
        i = np.array([t for t in range(P) if (t // m) % 2])[None, :]
        parts.append(((j // (2 * m) == i // (2 * m)) & ((j // m) % 2 == 0)) * 1.0)
    keep = np.ones((P, n_tiles))
    keep[:, n_tiles - 2] = 0.0
    return np.concatenate(parts + [keep], axis=1).astype(np.float32)


def kernel(**inputs):
    import numpy as _np
    import concourse.bacc as _bacc
    from concourse import mybir as _mybir
    from concourse.bass_utils import run_bass_kernel_spmd as _run

    nc = _bacc.Bacc("TRN2", target_bir_lowering=False, num_devices=1)
    arrays, args = {}, []
    named = {name: inputs[name] for name in _INS}
    named["masks"] = constants(inputs["L0_attn_x"].shape[1] // P)
    for name, value in named.items():
        a = _np.ascontiguousarray(value)
        arrays[f"in_{name}_dram"] = a
        args.append(nc.dram_tensor(f"in_{name}_dram", a.shape, _mybir.dt.from_np(a.dtype), kind="ExternalInput").ap())
    shape = inputs["L0_attn_x"].shape
    args.append(nc.dram_tensor("out_0_dram", shape, _mybir.dt.float32, kind="ExternalOutput").ap())
    adaln_kernel(nc, *args)
    r = _run(nc, [arrays], core_ids=[0])
    return r.results[0]["out_0_dram"]
```

```python
from contextlib import ExitStack

import concourse.bass as bass
from concourse import mybir

F32 = mybir.dt.float32
I32 = mybir.dt.int32
ALU = mybir.AluOpType
ACT = mybir.ActivationFunctionType

P = 128
PAIR = 2
LEVELS = 7
KS = 4
GROUP = 512
LN_EXP = "natural_log_exp_and_others"
QK_SCALE = 2.0 ** 32
ROUND = 2.0 ** -40
EARLY = 3
SOFTPLUS_MAX = 40.0


def adaln_kernel(nc, x, norm1_w, wq, wk, wv, conv_q, conv_k, conv_v, f_a, f_b, A_log, dt_bias,
                 b_w, g_a, g_b, onorm_w, wo, norm2_w, w1, w2, w3, W1, W2, W3, c, wmod, masks_in,
                 out):
    B, S, D = x.shape
    HTOT = A_log.shape[0]
    FF = w1.shape[1]
    KD = D // P
    NT = S // P
    NP = HTOT // PAIR
    C = B * PAIR
    NG = B * S // GROUP
    GB = S // GROUP
    SUB = GROUP // P
    FT = FF // P
    HALF = P // 2
    N_STEPS = NP * NT
    assert (B, D, f_a.shape[1]) == (2, 256, P) and C * P == 512 and S % GROUP == 0

    ctx = ExitStack()
    with ctx:
        def sb(where, name, shape):
            return where.enter_context(nc.sbuf_tensor(name, shape, F32))

        in_use = []

        def sem(name):
            in_use.append(nc.alloc_semaphore(name=name))
            return in_use[-1]

        def end_phase():
            nc.all_engine_barrier()
            nc.clear_and_free_semaphores(list(in_use))
            nc.all_engine_barrier()
            in_use.clear()

        bank = [ctx.enter_context(nc.psum_tensor(f"bank{i}", [P, 512], F32)) for i in range(8)]

        ident = sb(ctx, "ident", [P, P])
        ones = sb(ctx, "ones", [P, P])
        eps6 = sb(ctx, "eps6", [P, 1])
        eps5 = sb(ctx, "eps5", [P, 1])
        qscale = sb(ctx, "qscale", [P, 1])
        mod = sb(ctx, "mod", [P, 6 * KD, B])
        Y = sb(ctx, "Y", [P, KD, B * S])
        modv = mod[:, :, :].rearrange("p (v k) b -> p v k b", v=6)
        SA, CA, GA, SB_, CB, GBv = range(6)

        mid = ExitStack()
        hn = sb(mid, "hn", [P, KD, B * S])
        hfa = sb(mid, "hfa", [P, B * S])
        hga = sb(mid, "hga", [P, B * S])
        beta = sb(mid, "beta", [P, B * NT, HTOT])
        negA = sb(mid, "negA", [P, HTOT])
        masks = sb(mid, "masks", [P, LEVELS, HALF])
        keep = sb(mid, "keep", [P, NT])
        onw = sb(mid, "onw", [P, 1])

        with ExitStack() as ph:
            xs = sb(ph, "xs", [P, B * S // P, D])
            wm = sb(ph, "wm", [P, KD, 6 * D])
            fa_s = sb(ph, "fa_s", [P, KD, P])
            ga_s = sb(ph, "ga_s", [P, KD, P])
            bw_s = sb(ph, "bw_s", [P, KD, HTOT])
            n1 = sb(ph, "n1", [P, KD])
            cT = sb(ph, "cT", [P, KD, B])
            sgn = sb(ph, "sgn", [P, KD, B])
            mag = sb(ph, "mag", [P, KD, B])
            stats = sb(ph, "stats", [P, SUB, 6])
            mv = sb(ph, "mv", [P, SUB, 2])
            rs = sb(ph, "rs", [P, SUB])
            xh = sb(ph, "xh", [P, SUB, D])
            sq = sb(ph, "sq", [P, KD, GROUP])
            rr = sb(ph, "rr", [P, GROUP])
            bT = sb(ph, "bT", [HTOT, GROUP])
            b1 = sb(ph, "b1", [P, SUB, HTOT])

            load_c = sem("load_c")
            load_x = sem("load_x")
            load_w = sem("load_w")
            consts = sem("consts")
            silu_c = sem("silu_c")
            mod_mm = sem("mod_mm")
            mod_cp = sem("mod_cp")
            mod_steps = sem("mod_steps")
            negA_e = sem("negA_e")
            st_bn = sem("st_bn")
            st_mv = sem("st_mv")
            st_ln = sem("st_ln")
            st_rs = sem("st_rs")
            x_hat = sem("x_hat")
            x_tr = sem("x_tr")
            h_done = sem("h_done")
            h_sq = sem("h_sq")
            ss_mm = sem("ss_mm")
            ss_ln = sem("ss_ln")
            ss_rs = sem("ss_rs")
            hn_done = sem("hn_done")
            low_mm = sem("low_mm")
            b_mm = sem("b_mm")
            fa_cp = sem("fa_cp")
            ga_cp = sem("ga_cp")
            b_exp = sem("b_exp")
            b_tr = sem("b_tr")
            b_add = sem("b_add")
            b_done = sem("b_done")

            waited = sem("waited")
            N_C = 16 * 3
            N_W = 16 * 8

            with nc.Block() as block:
                @block.sync
                def _(eng):
                    with nc.allow_non_contiguous_dma("a few vectors, once"):
                        for b in range(B):
                            eng.dma_start(cT[:, :, b], c[b, :].rearrange("(k p) -> p k", p=P)).then_inc(load_c, 16)
                        eng.dma_start(wm[:, :, :], wmod.rearrange("(k p) n -> p k n", p=P)).then_inc(load_c, 16)
                        eng.dma_start(n1[:, :], norm1_w.rearrange("(k p) -> p k", p=P)).then_inc(load_w, 16)
                        eng.dma_start(onw[:, :], onorm_w.rearrange("(p a) -> p a", a=1)).then_inc(load_w, 16)
                        eng.dma_start(negA[:, :], A_log.rearrange("(a h) -> a h", a=1).broadcast_to([P, HTOT])).then_inc(load_w, 16)
                        for s_, d_ in ((fa_s, f_a), (ga_s, g_a), (bw_s, b_w)):
                            eng.dma_start(s_[:, :, :], d_.rearrange("(k p) n -> p k n", p=P)).then_inc(load_w, 16)
                        eng.dma_start(keep[:, :], masks_in[:, P + LEVELS * HALF:]).then_inc(load_w, 16)
                        eng.dma_start(masks[:, :, :], masks_in[:, P:P + LEVELS * HALF].rearrange("p (l n) -> p l n", l=LEVELS)).then_inc(load_w, 16)

                @block.gpsimd
                def _(eng):
                    eng.dma_start(ident[:, :], masks_in[:, 0:P]).then_inc(load_x, 16)
                    for b in range(B):
                        eng.dma_start(xs[:, b * NT:(b + 1) * NT, :],
                                      x[b, :, :].rearrange("(t p) d -> p t d", p=P)).then_inc(load_x, 16)
                    eng.memset(ones[:, :], 1.0).then_inc(consts, 1)
                    eng.memset(eps6[:, :], 1e-6).then_inc(consts, 1)
                    eng.memset(eps5[:, :], 1e-5).then_inc(consts, 1)
                    eng.memset(qscale[:, :], float(-0.5 * 4.852030263919617 - 0.6931471805599453)).then_inc(consts, 1)

                @block.tensor
                def _(eng):
                    eng.wait_ge(load_c, N_C)
                    eng.wait_ge(silu_c, 1)
                    for j in range(6 * KD):
                        for k in range(KD):
                            mm = eng.matmul(bank[7][:, j * B:(j + 1) * B], wm[:, k, j * P:(j + 1) * P],
                                            cT[:, k, :], start=(k == 0), stop=(k == KD - 1))
                    mm.then_inc(mod_mm, 1)
                    eng.wait_ge(load_w, N_W)
                    eng.wait_ge(load_x, 48)
                    eng.wait_ge(consts, 4)
                    with eng.Fori(0, NG) as g:
                        tok = bass.ds(g * GROUP, GROUP)
                        eng.wait_ge(x_hat, g + 1)
                        for k in range(KD):
                            for s in range(SUB):
                                mm = eng.transpose(bank[k][:, s * P:(s + 1) * P], xh[:, s, k * P:(k + 1) * P], ident[:, :])
                        mm.then_inc(x_tr, 1)
                        eng.wait_ge(h_sq, g + 1)
                        for k in range(KD):
                            mm = eng.matmul(bank[2][:, :], ones[:, :], sq[:, k, :], start=(k == 0), stop=(k == KD - 1))
                        mm.then_inc(ss_mm, 1)
                        eng.wait_ge(hn_done, g + 1)
                        for k in range(KD):
                            eng.matmul(bank[3][:, :], fa_s[:, k, :], hn[:, k, tok], start=(k == 0), stop=(k == KD - 1))
                        for k in range(KD):
                            mm = eng.matmul(bank[4][:, :], ga_s[:, k, :], hn[:, k, tok], start=(k == 0), stop=(k == KD - 1))
                        mm.then_inc(low_mm, 1)
                        for k in range(KD):
                            mm = eng.matmul(bank[5][0:HTOT, :], bw_s[:, k, :], hn[:, k, tok], start=(k == 0), stop=(k == KD - 1))
                        mm.then_inc(b_mm, 1)
                        eng.wait_ge(b_exp, g + 1)
                        eng.sem_inc(waited, 1)
                        for s in range(SUB):
                            mm = eng.transpose(bank[6][:, s * HTOT:(s + 1) * HTOT], bT[:, s * P:(s + 1) * P],
                                               ident[0:HTOT, 0:HTOT])
                        mm.then_inc(b_tr, 1)

                @block.scalar
                def _(eng):
                    eng.wait_ge(load_c, N_C)
                    eng.activation(cT[:, :, :], cT[:, :, :], ACT.Silu).then_inc(silu_c, 1)
                    eng.wait_ge(load_w, N_W)
                    eng.preload_act_table_set(LN_EXP)
                    eng.activation(negA[:, :], negA[:, :], ACT.Exp).then_inc(negA_e, 1)
                    eng.wait_ge(consts, 4)
                    eng.wait_ge(mod_steps, 5)
                    with eng.Fori(0, NG) as g:
                        tok = bass.ds(g * GROUP, GROUP)
                        half = bass.ds(g // GB, 1)
                        eng.wait_ge(st_mv, g + 1)
                        eng.activation(rs[:, :], mv[:, :, 1], ACT.Ln, bias=eps5[:, :]).then_inc(st_ln, 1)
                        eng.wait_ge(st_ln, g + 1)
                        eng.activation(rs[:, :], rs[:, :], ACT.Exp, scale=-0.5).then_inc(st_rs, 1)
                        eng.wait_ge(x_tr, g + 1)
                        for k in range(KD):
                            a = eng.activation(Y[:, k, tok], bank[k][:, :], ACT.Identity,
                                               bias=modv[:, SA, k, half], scale=modv[:, CA, k, half])
                        a.then_inc(h_done, 1)
                        eng.wait_ge(h_done, g + 1)
                        eng.sem_inc(waited, 1)
                        eng.activation(sq[:, :, :], Y[:, :, tok], ACT.Square).then_inc(h_sq, 1)
                        eng.wait_ge(ss_mm, g + 1)
                        eng.activation(rr[:, :], bank[2][:, :], ACT.Ln, bias=eps6[:, :], scale=1.0 / D).then_inc(ss_ln, 1)
                        eng.wait_ge(ss_ln, g + 1)
                        eng.activation(rr[:, :], rr[:, :], ACT.Exp, scale=-0.5).then_inc(ss_rs, 1)
                        eng.wait_ge(b_mm, g + 1)
                        eng.activation(bT[:, :], bank[5][0:HTOT, :], ACT.Exp, scale=-1.0).then_inc(b_exp, 1)
                        eng.activation(hfa[:, tok], bank[3][:, :], ACT.Copy).then_inc(fa_cp, 1)

                @block.vector
                def _(eng):
                    eng.wait_ge(mod_mm, 1)
                    eng.tensor_copy(mod[:, :, :], bank[7][:, 0:6 * KD * B].rearrange("p (j b) -> p j b", b=B)).then_inc(mod_cp, 1)
                    eng.wait_ge(mod_cp, 1)
                    n = 0
                    for v in (CA, CB):
                        eng.tensor_scalar(modv[:, v, :, :], modv[:, v, :, :], 1.0, None, ALU.add).then_inc(mod_steps, 1)
                        n += 1
                    for v in (GA, GBv):
                        gv = modv[:, v, :, :]
                        eng.tensor_scalar(sgn[:, :, :], gv, 0.0, 2.0, ALU.is_ge, ALU.mult).then_inc(mod_cp, 1)
                        eng.scalar_tensor_tensor(mag[:, :, :], gv, -1.0, gv, ALU.mult, ALU.max).then_inc(mod_cp, 1)
                        eng.wait_ge(mod_cp, 3 * (n - 2) + 3)
                        eng.tensor_scalar(mag[:, :, :], mag[:, :, :], 0.25, None, ALU.max).then_inc(mod_cp, 1)
                        eng.wait_ge(mod_cp, 3 * (n - 2) + 4)
                        eng.scalar_tensor_tensor(gv, sgn[:, :, :], -1.0, mag[:, :, :], ALU.add, ALU.mult).then_inc(mod_steps, 1)
                        n += 1
                        eng.wait_ge(mod_steps, n)
                    eng.wait_ge(negA_e, 1)
                    eng.tensor_scalar(negA[:, :], negA[:, :], -1.0, None, ALU.mult).then_inc(mod_steps, 1)
                    eng.wait_ge(load_x, 48)
                    with eng.Fori(0, NG) as g:
                        tok = bass.ds(g * GROUP, GROUP)
                        for s in range(SUB):
                            eng.bn_stats(stats[:, s, :], xs[:, bass.ds(g * SUB + s, 1), :]).then_inc(st_bn, 1)
                        eng.wait_ge(st_bn, (g + 1) * SUB)
                        eng.sem_inc(waited, 1)
                        for s in range(SUB):
                            a = eng.bn_aggr(mv[:, s, :], stats[:, s, :])
                        a.then_inc(st_mv, 1)
                        eng.wait_ge(st_mv, g + 1)
                        eng.wait_ge(st_rs, g + 1)
                        for s in range(SUB):
                            a = eng.tensor_scalar(xh[:, s, :], xs[:, bass.ds(g * SUB + s, 1), :],
                                                  mv[:, s, 0:1], rs[:, s:s + 1], ALU.subtract, ALU.mult)
                        a.then_inc(x_hat, 1)
                        eng.wait_ge(ss_rs, g + 1)
                        for k in range(KD):
                            a = eng.scalar_tensor_tensor(hn[:, k, tok], Y[:, k, tok], n1[:, k:k + 1], rr[:, :],
                                                         ALU.mult, ALU.mult)
                        a.then_inc(hn_done, 1)
                        eng.wait_ge(low_mm, g + 1)
                        eng.tensor_copy(hga[:, tok], bank[4][:, :]).then_inc(ga_cp, 1)
                        eng.wait_ge(b_tr, g + 1)
                        eng.tensor_scalar(b1[:, :, :], bank[6][:, 0:SUB * HTOT].rearrange("p (s h) -> p s h", h=HTOT),
                                          1.0, None, ALU.add).then_inc(b_add, 1)
                        eng.wait_ge(b_add, g + 1)
                        eng.reciprocal(beta[:, bass.ds(g * SUB, SUB), :], b1[:, :, :]).then_inc(b_done, 1)

        end_phase()

        with mid:
            w_qkv = sb(mid, "w_qkv", [P, 3, KD, PAIR * P])
            w_fb = sb(mid, "w_fb", [P, PAIR * P])
            w_gb = sb(mid, "w_gb", [P, PAIR * P])
            w_o = sb(mid, "w_o", [P, PAIR, D])
            cw = sb(mid, "cw", [P, 3, PAIR, KS])
            dtp = sb(mid, "dtp", [P, PAIR])

            def tile4(name):
                return sb(mid, name, [P, C, P])

            raw = sb(mid, "raw", [P, 3, C, P + KS - 1])
            acc = sb(mid, "acc", [P, 3, C, P])
            qk = sb(mid, "qk", [P, 2, C, P])
            qs, ks, vs = qk[:, 0, :, :], qk[:, 1, :, :], tile4("vs")
            zp, zc, u, r = tile4("zp"), tile4("zc"), tile4("u"), tile4("r")
            lnw = zc
            a = tile4("a")
            k_sq = tile4("k_sq")
            lns = sb(mid, "lns", [P, 2 * C])
            cq_new = sb(mid, "cq_new", [P, C])
            n_new = sb(mid, "n_new", [P, C])
            rk2_new = sb(mid, "rk2_new", [P, C])
            cq, nk, Dk = (sb(mid, n_, [P, C]) for n_ in ("cq", "nk", "Dk"))
            QKF = sb(mid, "QKF", [P, 2, C, P])
            KB = tile4("KB")
            tot = [a] + [sb(mid, f"tot{1 << s}", [P, C, P >> s]) for s in range(1, LEVELS + 1)]
            Am = [tile4(f"Am{s}") for s in range(LEVELS)]
            Zm = [None] + [tile4(f"Zm{s}") for s in range(1, LEVELS)]
            inv, invT = tile4("inv"), tile4("invT")
            qkT = tile4("qkT")
            Vn, R, U, St, KBt = tile4("Vn"), tile4("R"), tile4("U"), tile4("St"), tile4("KBt")
            tg, z, zs, oT = tile4("tg"), tile4("z"), tile4("zs"), tile4("oT")
            q_sq = zs
            QFt, qkTt = tile4("QFt"), tile4("qkTt")
            cqt, Dkt, tott = (sb(mid, n_, [P, C]) for n_ in ("cqt", "Dkt", "tott"))
            hgs = sb(mid, "hgs", [P, B, P])
            ssq, w1s, w2s, lnv, rstd, fs = (sb(mid, n_, [P, C]) for n_ in ("ssq", "w1s", "w2s", "lnv", "rstd", "fs"))

            B_Q, B_K, B_L0, B_L1, B_Z, B_Y, B_S, B_O = range(8)

            def chains(i):
                return bank[i][:, :].rearrange("p (c n) -> p c n", c=C)

            def heads(ap):
                return ap.rearrange("p (b a) n -> p b a n", b=B)

            def blocks(ap, s):
                return ap.rearrange("p c (n two m) -> p c n two m", two=2, m=1 << s)

            def odd1(t_, ch, s):
                return blocks(t_[:, :, :], s)[:, ch, :, 1, :]

            def even1(t_, ch, s):
                return blocks(t_[:, :, :], s)[:, ch, :, 0, :]

            def msk(s):
                return masks[:, s, :].rearrange("p (n m) -> p n m", m=1 << s)

            wf_in, wg_in, wo_in = sem("wf_in"), sem("wg_in"), sem("wo_in")
            proj = [sem(f"proj_{n_}") for n_ in "qkv"]
            proj_z = sem("proj_z")
            raw_cp = [sem(f"raw_{n_}") for n_ in "qkv"]
            taps = [[sem(f"tap{j}_{n_}") for j in range(3)] for n_ in "qkv"]
            silu_raw, silu_qk, silu_v = sem("silu_raw"), sem("silu_qk"), sem("silu_v")
            silu = [silu_qk, silu_qk, silu_v]
            halo = sem("halo")
            z_in, z_clip, u_exp, r_rnd, u_minus_r, ln_w, sp_sum, sp_max, a_exp = (
                sem(n_) for n_ in ("z_in", "z_clip", "u_exp", "r_rnd", "u_minus_r", "ln_w", "sp_sum", "sp_max", "a_exp"))
            sq_q, sq_k, norms_mm, norms_ln, norms_out = (
                sem(n_) for n_ in ("sq_q", "sq_k", "norms_mm", "norms_ln", "norms_out"))
            lvl0_mm, inv_tr, v_tr, gate_mm, kb_tr = (sem(n_) for n_ in ("lvl0_mm", "inv_tr", "v_tr", "gate_mm", "kb_tr"))
            lvl_mm = [sem(f"lvl_mm{s}") for s in range(LEVELS)]
            norms_in, qk_init, lvl0_cp, v_n = (sem(n_) for n_ in ("norms_in", "qk_init", "lvl0_cp", "v_n"))
            qk_raw = sem("qk_raw")
            qk_up = [sem(f"qk_up{s}") for s in range(LEVELS)]
            lvl_a = [sem(f"lvl_a{s}") for s in range(LEVELS)]
            lvl_q = [sem(f"lvl_q{s}") for s in range(LEVELS)]
            hg_cp, kb_init, gate_t, kb_cp, qf_cp, qkt_cp = (
                sem(n_) for n_ in ("hg_cp", "kb_init", "gate_t", "kb_cp", "qf_cp", "qkt_cp"))
            kb_raw = [sem(f"kb_raw{s}") for s in range(LEVELS)]
            kb_up = [sem(f"kb_up{s}") for s in range(LEVELS)]
            tots = [sem(f"tots{s}") for s in range(1, LEVELS + 1)]
            owner = {}

            def tail_ev(name, who):
                owner.setdefault(who, []).append(sem(name))
                return owner[who][-1]

            def inverse_ev(name, who):
                return [tail_ev(f"{name}{s}", who) if s > EARLY else sem(f"{name}{s}") for s in range(LEVELS)]

            z_mm, y_mm = inverse_ev("z_mm", "pe"), inverse_ev("y_mm", "pe")
            inv_m, z_cp = inverse_ev("inv_m", "dve"), inverse_ev("z_cp", "act")
            e_mm, w_mm, o_mm, s_mm, o_tr, wo_mm = (tail_ev(n_, "pe") for n_ in ("e_mm", "w_mm", "o_mm", "s_mm", "o_tr", "wo_mm"))
            tail_in, r_sub, u_mul, s_up, z_gate, ssq_w, ssq_w2, f_mul, y_add = (
                tail_ev(n_, "dve") for n_ in ("tail_in", "r_sub", "u_mul", "s_up", "z_gate", "ssq_w", "ssq_w2", "f_mul", "y_add"))
            zs_mul = tail_ev("zs_mul", "pool")
            ssq_sum, ln_v, r_std, oT_cp = (tail_ev(n_, "act") for n_ in ("ssq_sum", "ln_v", "r_std", "oT_cp"))
            s_zero = sem("s_zero")
            zeroed = sem("zeroed")
            waited = sem("waited2")

            def L(tile):
                return tile + 1

            def T(tile):
                return tile + 2

            def inv_count(s, tile):
                return T(tile) if s > EARLY else L(tile)

            def start_counts(eng, who):
                for e_ in owner[who]:
                    eng.sem_inc(e_, 1)

            NFW = 8
            wqkv_d = [w_.rearrange("(k p) n -> p k n", p=P) for w_ in (wq, wk, wv)]
            conv_d = [w_.rearrange("(h p) j -> p h j", p=P) for w_ in (conv_q, conv_k, conv_v)]
            dt_d = dt_bias.rearrange("(h p) -> p h", p=P)
            wo_d = wo.rearrange("(h p) n -> p h n", p=P)
            hn_v = hn[:, :, :].rearrange("p k (b s) -> p k b s", b=B)
            hfa_v = hfa[:, :].rearrange("p (b s) -> p b s", b=B)
            hga_v = hga[:, :].rearrange("p (b s) -> p b s", b=B)
            beta_v = beta[:, :, :].rearrange("p (b t) h -> p b t h", b=B)
            Y_v = Y[:, :, :].rearrange("p k (b s) -> p k b s", b=B)

            with nc.Block() as block:
                @block.sync
                def _(eng):
                    def front_weights(p):
                        cols = bass.ds(p * (PAIR * P), PAIR * P)
                        for n_ in range(3):
                            eng.dma_start(w_qkv[:, n_, :, :], wqkv_d[n_][:, :, cols]).then_inc(wf_in, 16)
                        eng.dma_start(w_fb[:, :], f_b[:, cols]).then_inc(wf_in, 16)
                        with nc.allow_non_contiguous_dma("a few scalars of each channel"):
                            for n_ in range(3):
                                eng.dma_start(cw[:, n_, :, :], conv_d[n_][:, bass.ds(p * PAIR, PAIR), :]).then_inc(wf_in, 16)
                            eng.dma_start(dtp[:, :], dt_d[:, bass.ds(p * PAIR, PAIR)]).then_inc(wf_in, 16)

                    def gate_weights(p):
                        eng.dma_start(w_gb[:, :], g_b[:, bass.ds(p * (PAIR * P), PAIR * P)]).then_inc(wg_in, 16)

                    def out_weights(p):
                        eng.dma_start(w_o[:, :, :], wo_d[:, bass.ds(p * PAIR, PAIR), :]).then_inc(wo_in, 16)

                    def front_free(p):
                        for e_ in (proj[0], proj[1], proj[2], proj_z, z_in, taps[0][2], taps[1][2], taps[2][2]):
                            eng.wait_ge(e_, L(p * NT - 1))

                    front_weights(0)
                    gate_weights(0)
                    out_weights(0)
                    with eng.Fori(1, NP) as p:
                        front_free(p)
                        front_weights(p)
                        eng.wait_ge(gate_mm, L(p * NT - 1))
                        gate_weights(p)
                        eng.wait_ge(wo_mm, T(p * NT - 1))
                        out_weights(p)
                    front_free(NP)
                    front_weights(NP - 1)
                    eng.wait_ge(gate_mm, L(NP * NT - 1))
                    gate_weights(NP - 1)

                @block.tensor
                def _(eng):
                    def project(n_, tile, bk, waits):
                        for s_, v_ in waits:
                            eng.wait_ge(s_, v_)
                        for h in range(PAIR):
                            for k in range(KD):
                                mm = eng.matmul(heads(chains(bk))[:, :, h, :], w_qkv[:, n_, k, h * P:(h + 1) * P],
                                                hn_v[:, k, :, bass.ds(tile * P, P)], start=(k == 0), stop=(k == KD - 1))
                        mm.then_inc(proj[n_], 1)

                    def project_z(tile, now):
                        eng.wait_ge(raw_cp[1], now)
                        for h in range(PAIR):
                            mm = eng.matmul(heads(chains(B_K))[:, :, h, :], w_fb[:, h * P:(h + 1) * P],
                                            hfa_v[:, :, bass.ds(tile * P, P)], start=True, stop=True)
                        mm.then_inc(proj_z, 1)

                    def sum_squares(now):
                        eng.wait_ge(z_in, now)
                        for n_, (s_, sq_) in enumerate(((sq_q, q_sq), (sq_k, k_sq))):
                            eng.wait_ge(s_, now)
                            for ch in range(C):
                                mm = eng.matmul(bank[B_K][:, n_ * C + ch:n_ * C + ch + 1], sq_[:, ch, :], ones[:, 0:1],
                                                start=True, stop=True)
                        mm.then_inc(norms_mm, 1)

                    def level0():
                        for ch in range(C):
                            mm = eng.matmul(chains(B_L0)[:, ch, :], ks[:, ch, :], qs[:, ch, :], start=True, stop=True)
                        mm.then_inc(lvl0_mm, 1)

                    def level(s):
                        kb = ks if s == 0 else KB
                        bk = B_L1 if s % 2 == 0 else B_L0
                        for ch in range(C):
                            mm = eng.matmul(chains(bk)[:, ch, :], kb[:, ch, :],
                                            QKF[:, :, ch, :].rearrange("p f (n two m) -> p f n two m", two=2, m=1 << s)[:, :, :, 1, :],
                                            start=True, stop=True)
                        mm.then_inc(lvl_mm[s], 1)

                    def z_product(s, tile):
                        eng.wait_ge(lvl_a[s], L(tile))
                        eng.wait_ge(inv_m[s - 1], inv_count(s - 1, tile))
                        for ch in range(C):
                            mm = eng.matmul(bank[B_Z][:, ch * HALF:(ch + 1) * HALF], Am[s][:, ch, :], even1(inv, ch, s),
                                            start=True, stop=True)
                        mm.then_inc(z_mm[s], 1)

                    def y_product(s, tile):
                        eng.wait_ge(z_cp[s], inv_count(s, tile))
                        for ch in range(C):
                            mm = eng.matmul(bank[B_Y][:, ch * HALF:(ch + 1) * HALF], Zm[s][:, ch, :], odd1(invT, ch, s),
                                            start=True, stop=True)
                        if s < LEVELS - 1:
                            for ch in range(C):
                                mm = eng.matmul(bank[B_Y][:, (C + ch) * HALF:(C + ch + 1) * HALF], invT[:, ch, :],
                                                even1(Zm[s], ch, s), start=True, stop=True)
                        mm.then_inc(y_mm[s], 1)

                    def levels_ready(s, tile):
                        eng.wait_ge(kb_up[s - 1], L(tile))
                        eng.wait_ge(qk_up[s - 1], L(tile))
                        if s == 1:
                            eng.wait_ge(kb_init, L(tile))
                            eng.wait_ge(lvl0_cp, L(tile))
                        else:
                            eng.wait_ge(lvl_q[s - 2], L(tile))

                    def step(i, first=False):
                        j, f = i + 1, i + 2
                        tile = f % NT
                        if not first:
                            eng.wait_ge(qk_up[LEVELS - 1], L(i))
                            eng.wait_ge(gate_t, L(i))
                            eng.wait_ge(s_up, T(i - 1))
                            eng.wait_ge(s_zero, i // NT + 1)
                            for ch in range(C):
                                mm = eng.matmul(chains(B_S)[:, ch, :], QKF[:, 1, ch, :], St[:, ch, :], start=True, stop=True)
                            mm.then_inc(e_mm, 1)
                            z_product(4, i)
                        eng.wait_ge(silu[2], L(j))
                        eng.wait_ge(raw_cp[2], L(j))
                        for ch in range(C):
                            mm = eng.transpose(chains(B_Q)[:, ch, :], vs[:, ch, :], ident[:, :])
                        mm.then_inc(v_tr, 1)
                        eng.wait_ge(silu[0], L(j))
                        eng.wait_ge(silu[1], L(j))
                        if not first:
                            eng.wait_ge(kb_cp, L(i))
                        level0()
                        if not first:
                            y_product(4, i)
                            eng.wait_ge(lvl_q[LEVELS - 1], L(i))
                        eng.wait_ge(qk_init, L(j))
                        level(0)
                        if not first:
                            z_product(5, i)
                        eng.wait_ge(wf_in, (f // NT + 1) * (16 * NFW))
                        project(0, tile, B_Q, [(v_n, L(j))])
                        if not first:
                            y_product(5, i)
                        levels_ready(1, j)
                        level(1)
                        project(1, tile, B_K, [(norms_ln, L(j))])
                        if not first:
                            z_product(6, i)
                        levels_ready(2, j)
                        level(2)
                        if not first:
                            y_product(6, i)
                        project(2, tile, B_Q, [(raw_cp[0], L(f))])
                        if not first:
                            eng.wait_ge(inv_m[LEVELS - 1], T(i))
                            eng.wait_ge(r_sub, T(i))
                            for ch in range(C):
                                mm = eng.matmul(chains(B_S)[:, ch, :], invT[:, ch, :], R[:, ch, :], start=True, stop=True)
                            mm.then_inc(w_mm, 1)
                        levels_ready(3, j)
                        level(3)
                        eng.wait_ge(lvl_a[0], L(j))
                        for ch in range(C):
                            mm = eng.transpose(chains(B_Z)[:, ch, :], Am[0][:, ch, :], ident[:, :])
                        mm.then_inc(inv_tr, 1)
                        project_z(tile, L(f))
                        if not first:
                            eng.wait_ge(u_mul, T(i))
                            eng.wait_ge(qf_cp, L(i))
                            eng.wait_ge(qkt_cp, L(i))
                            eng.wait_ge(y_add, T(i - 1))
                            for ch in range(C):
                                eng.matmul(chains(B_O)[:, ch, :], QFt[:, ch, :], St[:, ch, :], start=True, stop=False)
                                mm = eng.matmul(chains(B_O)[:, ch, :], qkTt[:, ch, :], U[:, ch, :], start=False, stop=True)
                            mm.then_inc(o_mm, 1)
                            for ch in range(C):
                                mm = eng.matmul(chains(B_S)[:, ch, :], KBt[:, ch, :], U[:, ch, :], start=True, stop=True)
                            mm.then_inc(s_mm, 1)
                        levels_ready(4, j)
                        level(4)
                        z_product(1, j)
                        eng.wait_ge(hg_cp, L(j))
                        eng.wait_ge(s_up, T(i))
                        eng.wait_ge(wg_in, (j // NT + 1) * 16)
                        for b in range(B):
                            mm = eng.matmul(bank[B_S][:, b * PAIR * P:(b + 1) * PAIR * P], hgs[:, b, :], w_gb[:, :],
                                            start=True, stop=True)
                        mm.then_inc(gate_mm, 1)
                        y_product(1, j)
                        if not first:
                            eng.wait_ge(zs_mul, T(i))
                            for ch in range(C):
                                mm = eng.transpose(chains(B_O)[:, ch, :], zs[:, ch, :], ident[:, :])
                            mm.then_inc(o_tr, 1)
                        levels_ready(5, j)
                        level(5)
                        z_product(2, j)
                        if not first:
                            eng.wait_ge(oT_cp, T(i))
                            eng.wait_ge(wo_in, (i // NT + 1) * 16)
                            for k in range(KD):
                                for h in range(PAIR):
                                    mm = eng.matmul(bank[B_O][:, k * B * P:(k + 1) * B * P], w_o[:, h, k * P:(k + 1) * P],
                                                    heads(oT[:, :, :])[:, :, h, :], start=(h == 0), stop=(h == PAIR - 1))
                            mm.then_inc(wo_mm, 1)
                        levels_ready(6, j)
                        level(6)
                        y_product(2, j)
                        z_product(3, j)
                        y_product(3, j)
                        sum_squares(L(f))
                        eng.wait_ge(kb_up[LEVELS - 1], L(j))
                        eng.wait_ge(lvl_q[LEVELS - 2], L(j))
                        for ch in range(C):
                            mm = eng.transpose(chains(B_L0)[:, ch, :], KB[:, ch, :], ident[:, :])
                        mm.then_inc(kb_tr, 1)

                    start_counts(eng, "pe")
                    eng.wait_ge(zeroed, 2 * LEVELS)
                    eng.wait_ge(wf_in, 16 * NFW)
                    project(0, 0, B_Q, [])
                    project(1, 0, B_K, [])
                    project(2, 0, B_Q, [(raw_cp[0], 1)])
                    project_z(0, 1)
                    sum_squares(1)
                    step(-1, first=True)
                    with eng.Fori(0, N_STEPS) as i:
                        step(i)

                @block.scalar
                def _(eng):
                    def first_tile(tile):
                        return isinstance(tile, int) and tile == 0

                    def take_raw(n_, bk, now):
                        eng.wait_ge(proj[n_], now)
                        eng.wait_ge(halo, now)
                        eng.activation(raw[:, n_, :, KS - 1:], chains(bk), ACT.Copy)
                        for h in range(PAIR):
                            x_ = eng.activation(heads(acc[:, n_, :, :])[:, :, h, :], heads(chains(bk))[:, :, h, :], ACT.Copy,
                                                scale=cw[:, n_, h, KS - 1:KS])
                        x_.then_inc(raw_cp[n_], 1)

                    def take_z(now):
                        eng.wait_ge(proj_z, now)
                        for h in range(PAIR):
                            x_ = eng.activation(heads(zp[:, :, :])[:, :, h, :], heads(chains(B_K))[:, :, h, :], ACT.Identity,
                                                bias=dtp[:, h:h + 1])
                        x_.then_inc(z_in, 1)

                    def silus(tile):
                        now = L(tile)
                        if not first_tile(tile):
                            for e_ in (lvl_mm[0], qk_init, kb_up[0], kb_init, v_tr):
                                eng.wait_ge(e_, L(tile - 1))
                        eng.wait_ge(taps[0][2], now)
                        eng.wait_ge(taps[1][2], now)
                        eng.activation(acc[:, 0:2, :, :], acc[:, 0:2, :, :], ACT.Silu).then_inc(silu_raw, 1)
                        eng.wait_ge(taps[2][2], now)
                        eng.activation(vs[:, :, :], acc[:, 2, :, :], ACT.Silu).then_inc(silu_v, 1)
                        eng.wait_ge(silu_raw, now)
                        eng.activation(qk[:, :, :, :], acc[:, 0:2, :, :], ACT.Copy, scale=QK_SCALE).then_inc(silu_qk, 1)

                    def softplus_logs(now):
                        eng.preload_act_table_set(LN_EXP)
                        eng.wait_ge(z_clip, now)
                        eng.activation(u[:, :, :], zc[:, :, :], ACT.Exp).then_inc(u_exp, 1)
                        eng.wait_ge(u_exp, now)
                        eng.activation(lnw[:, :, :], u[:, :, :], ACT.Ln, bias=1.0).then_inc(ln_w, 1)

                    def decays(pair, tile):
                        now = L(tile)
                        eng.wait_ge(sp_max, now)
                        if not first_tile(tile):
                            for e_ in (qk_up[0], kb_up[0], tots[0]):
                                eng.wait_ge(e_, L(tile - 1))
                        for h in range(PAIR):
                            x_ = eng.activation(heads(a[:, :, :])[:, :, h, :], heads(r[:, :, :])[:, :, h, :], ACT.Exp,
                                                scale=negA[:, bass.ds(pair * PAIR + h, 1)])
                        x_.then_inc(a_exp, 1)

                    def norms(tile):
                        now = L(tile)
                        eng.wait_ge(norms_mm, now)
                        eng.activation(lns[:, :], bank[B_K][:, 0:2 * C], ACT.Ln, bias=eps6[:, :],
                                       scale=QK_SCALE ** -2).then_inc(norms_ln, 1)
                        eng.wait_ge(norms_ln, now)
                        if not first_tile(tile):
                            eng.wait_ge(norms_in, L(tile - 1))
                        eng.activation(cq_new[:, :], lns[:, 0:C], ACT.Exp, scale=-0.5, bias=qscale[:, :])
                        eng.activation(n_new[:, :], lns[:, C:], ACT.Exp, scale=0.5)
                        eng.activation(rk2_new[:, :], lns[:, C:], ACT.Exp, scale=-1.0).then_inc(norms_out, 1)

                    def take_zm(s, tile):
                        eng.wait_ge(z_mm[s], inv_count(s, tile))
                        eng.activation(blocks(Zm[s][:, :, :], s)[:, :, :, 0, :],
                                       bank[B_Z][:, 0:C * HALF].rearrange("p (c n m) -> p c n m", c=C, m=1 << s),
                                       ACT.Copy).then_inc(z_cp[s], 1)

                    def step(i, first=False):
                        j, f = i + 1, i + 2
                        if not first:
                            take_zm(4, i)
                            take_zm(5, i)
                        eng.wait_ge(wf_in, (f // NT + 1) * (16 * NFW))
                        take_raw(0, B_Q, L(f))
                        take_raw(1, B_K, L(f))
                        if not first:
                            take_zm(6, i)
                        take_raw(2, B_Q, L(f))
                        take_z(L(f))
                        if not first:
                            eng.wait_ge(z_gate, T(i))
                            for ch in range(C):
                                x_ = eng.activation(oT[:, ch, :], z[:, ch, :], ACT.Square, scale=QK_SCALE ** -2, accum_out=ssq[:, ch:ch + 1])
                            x_.then_inc(ssq_sum, 1)
                            eng.wait_ge(ssq_w2, T(i))
                            eng.activation(lnv[:, :], w2s[:, :], ACT.Ln, bias=eps6[:, :], scale=1.0 / P).then_inc(ln_v, 1)
                            eng.wait_ge(ln_v, T(i))
                            eng.activation(rstd[:, :], lnv[:, :], ACT.Exp, scale=-0.5).then_inc(r_std, 1)
                        take_zm(1, j)
                        if not first:
                            eng.wait_ge(o_tr, T(i))
                            eng.activation(oT[:, :, :], chains(B_O), ACT.Copy, scale=onw[:, :]).then_inc(oT_cp, 1)
                        eng.wait_ge(gate_mm, L(j))
                        if not first:
                            eng.wait_ge(z_gate, T(i))
                        eng.activation(tg[:, :, :], chains(B_S), ACT.Tanh, scale=0.5).then_inc(gate_t, 1)
                        silus(f)
                        take_zm(2, j)
                        softplus_logs(L(f))
                        eng.wait_ge(qk_up[LEVELS - 1], L(j))
                        if not first:
                            eng.wait_ge(o_mm, T(i))
                        eng.activation(QFt[:, :, :], QKF[:, 0, :, :], ACT.Copy).then_inc(qf_cp, 1)
                        take_zm(3, j)
                        decays((f // NT) % NP, f)
                        norms(f)
                        eng.wait_ge(kb_tr, L(j))
                        if not first:
                            eng.wait_ge(s_mm, T(i))
                        eng.activation(KBt[:, :, :], chains(B_L0), ACT.Copy).then_inc(kb_cp, 1)

                    start_counts(eng, "act")
                    eng.wait_ge(wf_in, 16 * NFW)
                    take_raw(0, B_Q, 1)
                    take_raw(1, B_K, 1)
                    take_raw(2, B_Q, 1)
                    take_z(1)
                    silus(0)
                    softplus_logs(1)
                    norms(0)
                    decays(0, 0)
                    step(-1, first=True)
                    with eng.Fori(0, N_STEPS) as i:
                        step(i)

                @block.gpsimd
                def _(eng):
                    def squares(now):
                        eng.wait_ge(silu[0], now)
                        eng.tensor_tensor(q_sq[:, :, :], qs[:, :, :], qs[:, :, :], ALU.mult).then_inc(sq_q, 1)
                        eng.wait_ge(silu[1], now)
                        eng.tensor_tensor(k_sq[:, :, :], ks[:, :, :], ks[:, :, :], ALU.mult).then_inc(sq_k, 1)

                    def softplus_low(now):
                        eng.wait_ge(r_rnd, now)
                        eng.wait_ge(ln_w, now)
                        eng.tensor_tensor(u[:, :, :], u[:, :, :], r[:, :, :], ALU.subtract).then_inc(u_minus_r, 1)
                        eng.wait_ge(u_minus_r, now)
                        eng.tensor_tensor(r[:, :, :], lnw[:, :, :], u[:, :, :], ALU.add).then_inc(sp_sum, 1)

                    def round_off(ap, done):
                        eng.tensor_scalar(ap, ap, ROUND, -ROUND, ALU.add, ALU.add).then_inc(done, 1)

                    start_counts(eng, "pool")
                    for s in range(LEVELS):
                        eng.memset(Am[s][:, :, :], 0.0).then_inc(zeroed, 1)
                    for s in range(1, LEVELS):
                        eng.memset(Zm[s][:, :, :], 0.0).then_inc(zeroed, 1)
                    eng.memset(raw[:, :, :, :], 0.0).then_inc(zeroed, 1)
                    squares(1)
                    softplus_low(1)

                    def step(i, first=False):
                        j, f = i + 1, i + 2
                        now = L(j)
                        for e_ in (silu[1], a_exp):
                            eng.wait_ge(e_, L(j))
                        if not first:
                            eng.wait_ge(kb_tr, L(i))
                        eng.tensor_tensor(blocks(KB[:, :, :], 0)[:, :, :, 0, 0], blocks(ks[:, :, :], 0)[:, :, :, 0, 0],
                                          blocks(a[:, :, :], 0)[:, :, :, 1, 0], ALU.mult).then_inc(kb_raw[0], 1)
                        eng.tensor_copy(blocks(KB[:, :, :], 0)[:, :, :, 1, :], blocks(ks[:, :, :], 0)[:, :, :, 1, :]).then_inc(kb_init, 1)
                        eng.wait_ge(kb_raw[0], now)
                        eng.sem_inc(waited, 1)
                        round_off(blocks(KB[:, :, :], 0)[:, :, :, 0, :], kb_up[0])
                        if not first:
                            eng.wait_ge(qk_up[LEVELS - 1], L(i))
                            eng.wait_ge(tail_in, T(i))
                        for s in range(LEVELS):
                            src = tot[s][:, :, :].rearrange("p c (n two) -> p c n two", two=2)
                            if s:
                                eng.wait_ge(tots[s - 1], now)
                            eng.tensor_tensor(tot[s + 1][:, :, :], src[:, :, :, 0], src[:, :, :, 1], ALU.mult).then_inc(tots[s], 1)
                        if not first:
                            eng.wait_ge(gate_mm, L(i))
                        eng.tensor_copy(hgs[:, :, :], hga_v[:, :, bass.ds((j % NT) * P, P)]).then_inc(hg_cp, 1)
                        for s in range(1, LEVELS):
                            if s == 5 and not first:
                                eng.wait_ge(norms_mm, L(j))
                                eng.wait_ge(f_mul, T(i))
                                eng.tensor_tensor(zs[:, :, :], z[:, :, :], fs[:, :].unsqueeze(2).to_broadcast([P, C, P]),
                                                  ALU.mult).then_inc(zs_mul, 1)
                            if s == LEVELS - 1:
                                if not first:
                                    eng.wait_ge(o_tr, T(i))
                                squares(L(f))
                            m = 1 << s
                            eng.wait_ge(lvl_mm[s], now)
                            eng.wait_ge(kb_up[s - 1], now)
                            if s == 1:
                                eng.wait_ge(kb_init, now)
                            t_ = tot[s][:, :, :].rearrange("p c (n two) -> p c n two", two=2)[:, :, :, 1:2]
                            e_ = blocks(KB[:, :, :], s)[:, :, :, 0, :]
                            eng.tensor_tensor(e_, e_, t_.to_broadcast([P, C, P // (2 * m), m]), ALU.mult).then_inc(kb_raw[s], 1)
                            eng.wait_ge(kb_raw[s], now)
                            eng.sem_inc(waited, 1)
                            round_off(e_, kb_up[s])
                        softplus_low(L(f))

                    step(-1, first=True)
                    with eng.Fori(0, N_STEPS) as i:
                        step(i)

                @block.vector
                def _(eng):
                    def tap(n_, j, now):
                        for h in range(PAIR):
                            dst = heads(acc[:, n_, :, :])[:, :, h, :]
                            x_ = eng.scalar_tensor_tensor(dst, heads(raw[:, n_, :, :])[:, :, h, KS - 2 - j:KS - 2 - j + P],
                                                          cw[:, n_, h, KS - 2 - j:KS - 1 - j], dst, ALU.mult, ALU.add)
                        x_.then_inc(taps[n_][j], 1)

                    def conv(n_, now):
                        eng.wait_ge(raw_cp[n_], now)
                        for j in range(3):
                            if j:
                                eng.wait_ge(taps[n_][j - 1], now)
                            tap(n_, j, now)

                    def next_halo(keep, now):
                        eng.wait_ge(taps[2][2], now)
                        eng.tensor_scalar(raw[:, :, :, 0:KS - 1], raw[:, :, :, P:], keep, None, ALU.mult).then_inc(halo, 1)

                    def clip_z(now):
                        eng.wait_ge(z_in, now)
                        eng.tensor_scalar(zc[:, :, :], zp[:, :, :], SOFTPLUS_MAX, None, ALU.min).then_inc(z_clip, 1)

                    def round_w(now):
                        eng.wait_ge(u_exp, now)
                        eng.tensor_scalar(r[:, :, :], u[:, :, :], 1.0, -1.0, ALU.add, ALU.add).then_inc(r_rnd, 1)

                    def softplus_max(now):
                        eng.wait_ge(sp_sum, now)
                        eng.tensor_tensor(r[:, :, :], r[:, :, :], zp[:, :, :], ALU.max).then_inc(sp_max, 1)

                    def level_products(s, now):
                        bk = B_L1 if s % 2 == 0 else B_L0
                        m = 1 << s
                        eng.wait_ge(lvl_q[s - 1] if s else lvl0_cp, now)
                        ps = chains(bk).rearrange("p c (f n m) -> p c f n m", f=2, m=m)
                        for ch in range(C):
                            x_ = eng.scalar_tensor_tensor(odd1(Am[s], ch, s), ps[:, ch, 1, :, :], Dk[:, ch:ch + 1], msk(s),
                                                          ALU.mult, ALU.mult)
                        x_.then_inc(lvl_a[s], 1)
                        eng.copy_predicated(blocks(qkT[:, :, :], s)[:, :, :, 1, :],
                                            msk(s).bitcast(I32).unsqueeze(1).to_broadcast([P, C, HALF // m, m]),
                                            ps[:, :, 0, :, :]).then_inc(lvl_q[s], 1)

                    def grow_f(s, now):
                        m = 1 << s
                        eng.wait_ge(lvl_mm[s], now)
                        if s:
                            eng.wait_ge(tots[s - 1], now)
                            eng.wait_ge(qk_up[s - 1], now)
                        else:
                            eng.wait_ge(qk_init, now)
                        t_ = tot[s][:, :, :].rearrange("p c (n two) -> p c n two", two=2)[:, :, :, 0:1]
                        for f in range(2):
                            o_ = blocks(QKF[:, f, :, :], s)[:, :, :, 1, :]
                            x_ = eng.tensor_tensor(o_, o_, t_.to_broadcast([P, C, P // (2 * m), m]), ALU.mult)
                        x_.then_inc(qk_raw, 1)
                        eng.wait_ge(qk_raw, (now - 1) * (LEVELS + 1) + s + 2)
                        o_ = QKF[:, :, :, :].rearrange("p f c n -> p (f c) n").rearrange("p c (n two m) -> p c n two m", two=2, m=m)[:, :, :, 1, :]
                        eng.tensor_scalar(o_, o_, ROUND, -ROUND, ALU.add, ALU.add).then_inc(qk_up[s], 1)

                    def grow_inverse(s, tile):
                        eng.wait_ge(y_mm[s], inv_count(s, tile))
                        eng.wait_ge(inv_m[s - 1], inv_count(s - 1, tile))
                        m = 1 << s
                        ps = bank[B_Y][:, :].rearrange("p (f c n m) -> p f c n m", f=2, c=C, m=m)
                        o_ = blocks(invT[:, :, :], s)[:, :, :, 1, :]
                        x_ = eng.tensor_tensor(o_, o_, ps[:, 0, :, :, :], ALU.subtract)
                        if s < LEVELS - 1:
                            e_ = blocks(inv[:, :, :], s)[:, :, :, 0, :]
                            x_ = eng.tensor_tensor(e_, e_, ps[:, 1, :, :, :], ALU.subtract)
                        x_.then_inc(inv_m[s], 1)

                    identb = ident[:, :].unsqueeze(1).to_broadcast([P, C, P])
                    start_counts(eng, "dve")
                    eng.wait_ge(zeroed, 2 * LEVELS)
                    eng.sem_inc(halo, 1)
                    eng.wait_ge(wf_in, 16 * NFW)
                    for n_ in range(3):
                        conv(n_, 1)
                    next_halo(1.0, 1)
                    clip_z(1)
                    round_w(1)
                    softplus_max(1)

                    def step(i, first=False):
                        j, f = i + 1, i + 2
                        lv, fr = L(j), L(f)
                        if not first:
                            for e_ in (u_mul, f_mul, s_up):
                                eng.wait_ge(e_, T(i - 1))
                            eng.wait_ge(tots[LEVELS - 1], L(i))
                            eng.tensor_copy(tott[:, :], tot[LEVELS][:, :, 0])
                            eng.tensor_copy(cqt[:, :], cq[:, :])
                            eng.tensor_copy(Dkt[:, :], Dk[:, :]).then_inc(tail_in, 1)
                            eng.wait_ge(lvl_a[LEVELS - 1], L(i))
                            eng.wait_ge(tail_in, T(i))
                        if not first:
                            eng.wait_ge(e_mm, T(i))
                            eng.wait_ge(v_n, L(i))
                            eng.tensor_tensor(R[:, :, :], Vn[:, :, :], chains(B_S), ALU.subtract).then_inc(r_sub, 1)
                            eng.wait_ge(qf_cp, L(i))
                        eng.wait_ge(silu[0], lv)
                        eng.wait_ge(a_exp, lv)
                        for f_, t_ in ((0, qs), (1, ks)):
                            x_ = eng.tensor_tensor(QKF[:, f_, :, :], t_[:, :, :], a[:, :, :], ALU.mult)
                        x_.then_inc(qk_raw, 1)
                        eng.wait_ge(qk_raw, j * (LEVELS + 1) + 1)
                        eng.tensor_scalar(QKF[:, :, :, :], QKF[:, :, :, :], ROUND, -ROUND, ALU.add, ALU.add).then_inc(qk_init, 1)
                        if not first:
                            grow_inverse(4, i)
                            eng.wait_ge(r_sub, T(i))
                        eng.wait_ge(norms_out, lv)
                        eng.tensor_copy(cq[:, :], cq_new[:, :])
                        eng.tensor_scalar(nk[:, :], n_new[:, :], QK_SCALE ** 2, None, ALU.mult)
                        eng.scalar_tensor_tensor(Dk[:, :].rearrange("p (b a) -> p b a", b=B),
                                                 rk2_new[:, :].rearrange("p (b a) -> p b a", b=B), QK_SCALE ** -2,
                                                 beta_v[:, :, bass.ds(j % NT, 1), bass.ds(((j // NT) % NP) * PAIR, PAIR)].rearrange("p b o a -> p b (o a)"),
                                                 ALU.mult, ALU.mult).then_inc(norms_in, 1)
                        eng.wait_ge(norms_in, lv)
                        eng.wait_ge(v_tr, lv)
                        eng.tensor_tensor(Vn[:, :, :], chains(B_Q), nk[:, :].unsqueeze(2).to_broadcast([P, C, P]),
                                          ALU.mult).then_inc(v_n, 1)
                        grow_f(0, lv)
                        if not first:
                            eng.wait_ge(qkt_cp, L(i))
                        eng.wait_ge(lvl0_mm, lv)
                        eng.tensor_tensor(qkT[:, :, :], chains(B_L0), identb, ALU.mult).then_inc(lvl0_cp, 1)
                        level_products(0, lv)
                        if not first:
                            grow_inverse(5, i)
                        grow_f(1, lv)
                        level_products(1, lv)
                        conv(0, fr)
                        grow_f(2, lv)
                        if not first:
                            grow_inverse(6, i)
                        level_products(2, lv)
                        if not first:
                            eng.wait_ge(w_mm, T(i))
                            eng.tensor_tensor(U[:, :, :], chains(B_S), Dkt[:, :].unsqueeze(2).to_broadcast([P, C, P]),
                                              ALU.mult).then_inc(u_mul, 1)
                            eng.tensor_tensor(w1s[:, :], cqt[:, :], cqt[:, :], ALU.mult).then_inc(ssq_w, 1)
                        conv(1, fr)
                        grow_f(3, lv)
                        eng.wait_ge(lvl_a[0], lv)
                        if not first:
                            eng.wait_ge(inv_m[LEVELS - 1], T(i))
                        eng.tensor_tensor(invT[:, :, :], identb, Am[0][:, :, :], ALU.subtract)
                        eng.wait_ge(inv_tr, lv)
                        eng.tensor_tensor(inv[:, :, :], identb, chains(B_Z), ALU.subtract).then_inc(inv_m[0], 1)
                        level_products(3, lv)
                        if not first:
                            eng.wait_ge(o_mm, T(i))
                            eng.scalar_tensor_tensor(z[:, :, :], tg[:, :, :], 1.0, chains(B_O), ALU.add, ALU.mult).then_inc(z_gate, 1)
                            eng.wait_ge(s_mm, T(i))
                            for ch in range(C):
                                x_ = eng.scalar_tensor_tensor(St[:, ch, :], St[:, ch, :], tott[:, ch:ch + 1], chains(B_S)[:, ch, :],
                                                              ALU.mult, ALU.add)
                            x_.then_inc(s_up, 1)
                            eng.wait_ge(ssq_sum, T(i))
                            eng.wait_ge(ssq_w, T(i))
                            eng.tensor_tensor(w2s[:, :], ssq[:, :], w1s[:, :], ALU.mult).then_inc(ssq_w2, 1)
                        conv(2, fr)
                        clip_z(fr)
                        grow_f(4, lv)
                        if not first:
                            eng.wait_ge(r_std, T(i))
                            eng.scalar_tensor_tensor(fs[:, :], cqt[:, :], QK_SCALE ** -2, rstd[:, :], ALU.mult, ALU.mult).then_inc(f_mul, 1)
                        level_products(4, lv)
                        grow_inverse(1, j)
                        grow_f(5, lv)
                        level_products(5, lv)
                        next_halo(1.0 if first else keep[:, bass.ds(i % NT, 1)], fr)
                        grow_f(6, lv)
                        grow_inverse(2, j)
                        round_w(fr)
                        level_products(6, lv)
                        if not first:
                            eng.wait_ge(wo_mm, T(i))
                            y_ = Y_v[:, :, :, bass.ds((i % NT) * P, P)]
                            eng.tensor_tensor(y_, y_, bank[B_O][:, :].rearrange("p (k b n) -> p k b n", k=KD, b=B),
                                              ALU.add).then_inc(y_add, 1)
                        softplus_max(fr)
                        grow_inverse(3, j)
                        eng.wait_ge(lvl_q[LEVELS - 1], lv)
                        eng.tensor_scalar(qkTt[:, :, :], qkT[:, :, :], ROUND, -ROUND, ALU.add, ALU.add).then_inc(qkt_cp, 1)

                    step(-1, first=True)
                    with eng.Fori(0, NP) as pair:
                        eng.memset(St[:, :, :], 0.0).then_inc(s_zero, 1)
                        with eng.Fori(0, NT) as t:
                            step(pair * NT + t)

        end_phase()

        with ExitStack() as ph:
            xt = sb(ph, "xt", [P, SUB, D])
            w1_s, w3_s = sb(ph, "w1_s", [P, KD, FF]), sb(ph, "w3_s", [P, KD, FF])
            w2_s = sb(ph, "w2_s", [P, FT, D])
            W1T, W3T = sb(ph, "W1T", [P, KD, FF]), sb(ph, "W3T", [P, KD, FF])
            W2T = sb(ph, "W2T", [P, FT, D])
            W1n, W3n = sb(ph, "W1n", [P, FT, D]), sb(ph, "W3n", [P, FT, D])
            W2n = [sb(ph, f"W2n{i}", [P, KD, FF]) for i in range(2)]
            n2 = sb(ph, "n2", [P, KD])
            def tile2(name):
                return sb(ph, name, [P, KD, GROUP])
            sq, h2, ao, x3, dev, h3, x4 = (tile2(n_) for n_ in ("sq3", "h2", "ao", "x3", "dev", "h3", "x4"))
            rr = sb(ph, "rr3", [P, GROUP])
            sg = sb(ph, "sg", [P, 2, GROUP])
            G = sb(ph, "G", [P, FT, GROUP])
            ot = sb(ph, "ot", [P, SUB, D])

            ld_w, ld_x, st_o = sem("ld_w3"), sem("ld_x3"), sem("st_out")
            had, w_tr, w_cp = sem("had"), sem("w_tr"), sem("w_cp")
            sq1, sum1, ln1, rs1, h2_ok = (sem(n_) for n_ in ("sq1", "sum1", "ln1", "rs1", "h2_ok"))
            up, act_ok, g_ok, down = ([sem(f"{n_}{j}") for j in range(2)] for n_ in ("up", "silu_ok", "g_ok", "down"))
            ao_ok, xT_mm, x3_ok, sum2, dev_ok, sq2, sum3, ln2, rs2, nrm_ok, h3_ok, x4_ok, oT_mm, ot_ok = (
                sem(n_) for n_ in ("ao_ok", "xT_mm", "x3_ok", "sum2", "dev_ok", "sq2", "sum3", "ln2", "rs2", "nrm_ok",
                                   "h3_ok", "x4_ok", "oT_mm", "ot_ok"))
            N_HAD = FF.bit_length() - 1
            out_v = out.rearrange("b (g s p) d -> (b g) p s d", s=SUB, p=P)
            x_v = x.rearrange("b (g s p) d -> (b g) p s d", s=SUB, p=P)

            with nc.Block() as block:
                @block.sync
                def _(eng):
                    for s_, d_ in ((w1_s, w1), (w3_s, w3)):
                        eng.dma_start(s_[:, :, :], d_.rearrange("(k p) n -> p k n", p=P)).then_inc(ld_w, 16)
                    for s_, d_ in ((w2_s, w2), (W1n, W1), (W3n, W3)):
                        eng.dma_start(s_[:, :, :], d_.rearrange("(f p) n -> p f n", p=P)).then_inc(ld_w, 16)
                    eng.dma_start(W2n[0][:, :, :], W2.rearrange("(k p) n -> p k n", p=P)).then_inc(ld_w, 16)
                    with nc.allow_non_contiguous_dma("a vector, once"):
                        eng.dma_start(n2[:, :], norm2_w.rearrange("(k p) -> p k", p=P)).then_inc(ld_w, 16)
                    eng.dma_start(xt[:, :, :], x_v[0]).then_inc(ld_x, 16)
                    with eng.Fori(0, NG) as g:
                        eng.wait_ge(ot_ok, g + 1)
                        eng.dma_start(out_v[bass.ds(g, 1)].rearrange("o p s d -> p (o s) d"), ot[:, :, :]).then_inc(st_o, 16)
                        eng.wait_ge(xT_mm, g + 1)
                        eng.dma_start(xt[:, :, :], x_v[bass.ds((g + 1) % NG, 1)].rearrange("o p s d -> p (o s) d")).then_inc(ld_x, 16)
                    eng.wait_ge(st_o, 16 * NG)
                    eng.wait_ge(ld_x, 16 * (NG + 1))

                @block.tensor
                def _(eng):
                    eng.wait_ge(ld_w, 16 * 7)
                    n = 0
                    for src, dst in ((W1n, W1T), (W3n, W3T)):
                        for k in range(KD):
                            for q_ in range(FT // 4):
                                if n >= 4:
                                    eng.wait_ge(w_cp, n - 3)
                                for f in range(4):
                                    mm = eng.transpose(bank[n % 4][:, f * P:(f + 1) * P], src[:, q_ * 4 + f, k * P:(k + 1) * P], ident[:, :])
                                mm.then_inc(w_tr, 1)
                                n += 1
                    eng.wait_ge(had, 2 * N_HAD)
                    Wh = W2n[N_HAD % 2]
                    for f2 in range(FT // 2):
                        eng.wait_ge(w_cp, n - 3)
                        for f in range(2):
                            for k in range(KD):
                                mm = eng.transpose(bank[n % 4][:, (f * KD + k) * P:(f * KD + k + 1) * P],
                                                   Wh[:, k, (f2 * 2 + f) * P:(f2 * 2 + f + 1) * P], ident[:, :])
                        mm.then_inc(w_tr, 1)
                        n += 1
                    eng.wait_ge(w_cp, n)

                    def feed_forward(j, wa, wb, wd, src, g):
                        for f in range(FT):
                            if f >= 2:
                                eng.wait_ge(g_ok[j], g * FT + f - 1)
                            for bk, w_ in ((f % 2, wa), (2 + f % 2, wb)):
                                for k in range(KD):
                                    mm = eng.matmul(bank[bk][:, :], w_[:, k, f * P:(f + 1) * P], src[:, k, :],
                                                    start=(k == 0), stop=(k == KD - 1))
                            mm.then_inc(up[j], 1)
                        eng.wait_ge(g_ok[j], (g + 1) * FT)
                        for k in range(KD):
                            for f in range(FT):
                                mm = eng.matmul(bank[4 + k][:, :], wd[:, f, k * P:(k + 1) * P], G[:, f, :],
                                                start=(f == 0), stop=(f == FT - 1))
                        mm.then_inc(down[j], 1)

                    with eng.Fori(0, NG) as g:
                        eng.wait_ge(sq1, g + 1)
                        for k in range(KD):
                            mm = eng.matmul(bank[2][:, :], ones[:, :], sq[:, k, :], start=(k == 0), stop=(k == KD - 1))
                        mm.then_inc(sum1, 1)
                        eng.wait_ge(ld_x, 16 * (g + 1))
                        for k in range(KD):
                            for s in range(SUB):
                                mm = eng.transpose(bank[6 + k][:, s * P:(s + 1) * P], xt[:, s, k * P:(k + 1) * P], ident[:, :])
                        mm.then_inc(xT_mm, 1)
                        eng.wait_ge(h2_ok, g + 1)
                        feed_forward(0, w1_s, w3_s, w2_s, h2, g)
                        eng.wait_ge(x3_ok, g + 1)
                        for k in range(KD):
                            mm = eng.matmul(bank[2][:, :], ones[:, :], x3[:, k, :], start=(k == 0), stop=(k == KD - 1))
                        mm.then_inc(sum2, 1)
                        eng.wait_ge(sq2, g + 1)
                        for k in range(KD):
                            mm = eng.matmul(bank[3][:, :], ones[:, :], sq[:, k, :], start=(k == 0), stop=(k == KD - 1))
                        mm.then_inc(sum3, 1)
                        eng.wait_ge(h3_ok, g + 1)
                        feed_forward(1, W1T, W3T, W2T, h3, g)
                        eng.wait_ge(x4_ok, g + 1)
                        for k in range(KD):
                            for s in range(SUB):
                                mm = eng.transpose(bank[6 + k][:, s * P:(s + 1) * P], x4[:, k, s * P:(s + 1) * P], ident[:, :])
                        mm.then_inc(oT_mm, 1)
                        eng.wait_ge(ot_ok, g + 1)

                @block.scalar
                def _(eng):
                    def silu_up(j, g):
                        for f in range(FT):
                            eng.wait_ge(up[j], g * FT + f + 1)
                            if f >= 2:
                                eng.wait_ge(g_ok[j], g * FT + f - 1)
                            eng.activation(sg[:, f % 2, :], bank[f % 2][:, :], ACT.Silu).then_inc(act_ok[j], 1)

                    with eng.Fori(0, NG) as g:
                        tok = bass.ds(g * GROUP, GROUP)
                        half = bass.ds(g // GB, 1)
                        eng.activation(sq[:, :, :], Y[:, :, tok], ACT.Square).then_inc(sq1, 1)
                        eng.preload_act_table_set(LN_EXP)
                        eng.wait_ge(sum1, g + 1)
                        eng.activation(rr[:, :], bank[2][:, :], ACT.Ln, bias=eps6[:, :], scale=1.0 / D).then_inc(ln1, 1)
                        eng.wait_ge(ln1, g + 1)
                        eng.activation(rr[:, :], rr[:, :], ACT.Exp, scale=-0.5).then_inc(rs1, 1)
                        silu_up(0, g)
                        eng.wait_ge(dev_ok, g + 1)
                        eng.activation(sq[:, :, :], dev[:, :, :], ACT.Square).then_inc(sq2, 1)
                        eng.preload_act_table_set(LN_EXP)
                        eng.wait_ge(sum3, g + 1)
                        eng.activation(rr[:, :], bank[3][:, :], ACT.Ln, bias=eps5[:, :], scale=1.0 / D).then_inc(ln2, 1)
                        eng.wait_ge(ln2, g + 1)
                        eng.activation(rr[:, :], rr[:, :], ACT.Exp, scale=-0.5).then_inc(rs2, 1)
                        eng.wait_ge(nrm_ok, g + 1)
                        for k in range(KD):
                            x_ = eng.activation(h3[:, k, :], dev[:, k, :], ACT.Identity,
                                                bias=modv[:, SB_, k, half], scale=modv[:, CB, k, half])
                        x_.then_inc(h3_ok, 1)
                        silu_up(1, g)
                        eng.wait_ge(oT_mm, g + 1)
                        for k in range(KD):
                            x_ = eng.activation(ot[:, :, k * P:(k + 1) * P], bank[6 + k][:, :].rearrange("p (s n) -> p s n", n=P), ACT.Copy)
                        x_.then_inc(ot_ok, 1)

                @block.vector
                def _(eng):
                    eng.wait_ge(ld_w, 16 * 7)
                    for j in range(N_HAD):
                        src, dst = (W2n[j % 2], W2n[(j + 1) % 2])
                        sv, dv = (t_[:, :, :].rearrange("p k (n two m) -> p (k n) two m", two=2, m=1 << j) for t_ in (src, dst))
                        if j:
                            eng.wait_ge(had, 2 * j)
                        eng.tensor_tensor(dv[:, :, 0, :], sv[:, :, 0, :], sv[:, :, 1, :], ALU.add).then_inc(had, 1)
                        eng.tensor_tensor(dv[:, :, 1, :], sv[:, :, 0, :], sv[:, :, 1, :], ALU.subtract).then_inc(had, 1)
                    n = 0
                    for dst in (W1T, W3T):
                        for k in range(KD):
                            for q_ in range(FT // 4):
                                eng.wait_ge(w_tr, n + 1)
                                eng.tensor_copy(dst[:, k, q_ * 512:(q_ + 1) * 512], bank[n % 4][:, :]).then_inc(w_cp, 1)
                                n += 1
                    for f2 in range(FT // 2):
                        eng.wait_ge(w_tr, n + 1)
                        eng.tensor_scalar(W2T[:, f2 * 2:f2 * 2 + 2, :], bank[n % 4][:, :].rearrange("p (f n) -> p f n", f=2),
                                          float(FF) ** -0.5, None, ALU.mult).then_inc(w_cp, 1)
                        n += 1

                    def gate_up(j, g):
                        for f in range(FT):
                            eng.wait_ge(act_ok[j], g * FT + f + 1)
                            eng.tensor_tensor(G[:, f, :], sg[:, f % 2, :], bank[2 + f % 2][:, :], ALU.mult).then_inc(g_ok[j], 1)

                    with eng.Fori(0, NG) as g:
                        tok = bass.ds(g * GROUP, GROUP)
                        half = bass.ds(g // GB, 1)
                        eng.wait_ge(rs1, g + 1)
                        for k in range(KD):
                            x_ = eng.scalar_tensor_tensor(h2[:, k, :], Y[:, k, tok], n2[:, k:k + 1], rr[:, :], ALU.mult, ALU.mult)
                        x_.then_inc(h2_ok, 1)
                        gate_up(0, g)
                        eng.wait_ge(down[0], g + 1)
                        for k in range(KD):
                            x_ = eng.tensor_tensor(ao[:, k, :], Y[:, k, tok], bank[4 + k][:, :], ALU.add)
                        x_.then_inc(ao_ok, 1)
                        eng.wait_ge(ao_ok, g + 1)
                        eng.wait_ge(xT_mm, g + 1)
                        for k in range(KD):
                            x_ = eng.scalar_tensor_tensor(x3[:, k, :], ao[:, k, :], modv[:, GA, k, half], bank[6 + k][:, :],
                                                          ALU.mult, ALU.add)
                        x_.then_inc(x3_ok, 1)
                        eng.wait_ge(x3_ok, g + 1)
                        eng.wait_ge(sum2, g + 1)
                        for k in range(KD):
                            x_ = eng.scalar_tensor_tensor(dev[:, k, :], bank[2][:, :], -1.0 / D, x3[:, k, :], ALU.mult, ALU.add)
                        x_.then_inc(dev_ok, 1)
                        eng.wait_ge(dev_ok, g + 1)
                        eng.wait_ge(rs2, g + 1)
                        for k in range(KD):
                            x_ = eng.tensor_tensor(dev[:, k, :], dev[:, k, :], rr[:, :], ALU.mult)
                        x_.then_inc(nrm_ok, 1)
                        gate_up(1, g)
                        eng.wait_ge(down[1], g + 1)
                        for k in range(KD):
                            x_ = eng.scalar_tensor_tensor(x4[:, k, :], bank[4 + k][:, :], modv[:, GBv, k, half], x3[:, k, :],
                                                          ALU.mult, ALU.add)
                        x_.then_inc(x4_ok, 1)


_INS = ["L0_attn_x", "L0_attn_norm1_w", "L0_attn_wq", "L0_attn_wk", "L0_attn_wv", "L0_attn_conv_q", "L0_attn_conv_k",
        "L0_attn_conv_v", "L0_attn_f_a", "L0_attn_f_b", "L0_attn_A_log", "L0_attn_dt_bias", "L0_attn_b_w",
        "L0_attn_g_a", "L0_attn_g_b", "L0_attn_onorm_w", "L0_attn_wo", "L0_attn_norm2_w", "L0_attn_w1", "L0_attn_w2",
        "L0_attn_w3", "L0_ffn_W1", "L0_ffn_W2", "L0_ffn_W3", "L0_c", "L0_wmod"]


def constants(n_tiles):
    import numpy as np

    j = np.arange(P)[:, None]
    parts = [np.eye(P)]
    for s in range(LEVELS):
        m = 1 << s
        i = np.array([t for t in range(P) if (t // m) % 2])[None, :]
        parts.append(((j // (2 * m) == i // (2 * m)) & ((j // m) % 2 == 0)) * 1.0)
    keep = np.ones((P, n_tiles))
    keep[:, n_tiles - 3] = 0.0
    return np.concatenate(parts + [keep], axis=1).astype(np.float32)


def kernel(**inputs):
    import numpy as _np
    import concourse.bacc as _bacc
    from concourse import mybir as _mybir
    from concourse.bass_utils import run_bass_kernel_spmd as _run

    nc = _bacc.Bacc("TRN2", target_bir_lowering=False, num_devices=1)
    arrays, args = {}, []
    named = {name: inputs[name] for name in _INS}
    named["masks"] = constants(inputs["L0_attn_x"].shape[1] // P)
    for name, value in named.items():
        a = _np.ascontiguousarray(value)
        arrays[f"in_{name}_dram"] = a
        args.append(nc.dram_tensor(f"in_{name}_dram", a.shape, _mybir.dt.from_np(a.dtype), kind="ExternalInput").ap())
    shape = inputs["L0_attn_x"].shape
    args.append(nc.dram_tensor("out_0_dram", shape, _mybir.dt.float32, kind="ExternalOutput").ap())
    adaln_kernel(nc, *args)
    r = _run(nc, [arrays], core_ids=[0])
    return r.results[0]["out_0_dram"]
```
